# Optimizing a Trainium2 kernel written in Bass

```python
import numpy as np
import jax
import jax.numpy as jnp

def _softmax(x, axis=-1):
    return jax.nn.softmax(x, axis=axis)

def _gelu(x):
    return jax.nn.gelu(x, approximate=True)

def _silu(x):
    return jax.nn.silu(x)

def _sigmoid(x):
    return jax.nn.sigmoid(x)

def _layernorm(x, axis=-1, eps=1e-05):
    m = jnp.mean(x, axis=axis, keepdims=True)
    v = jnp.var(x, axis=axis, keepdims=True)
    return (x - m) / jnp.sqrt(v + eps)

def _scatter_add(tgt, idx, src, axis=0):
    return tgt.at[idx].add(src)

def _segment_sum(src, seg, n):
    return jax.ops.segment_sum(src, seg, n)
kernel_name = 'mk_adaln_ffn_d2_seqx_r4_3d198b'

def setup_inputs(seed: int=0):
    np.random.seed(seed)
    _w = jnp.asarray

    def _rec_inputs():
        import jax
        import jax.numpy as jnp
        _rk = jax.random.key(seed)
        x = -0.000125 + 0.9999 * jax.random.normal(jax.random.fold_in(_rk, 1), (32, 64, 1024), jnp.float32)
        _lenS = 64 - jax.random.randint(jax.random.fold_in(_rk, 7), (32,), 0, max(1, 64 // 4) + 1, jnp.int32)
        _lenS2 = 64 - jax.random.randint(jax.random.fold_in(_rk, 8), (32,), 0, max(1, 64 // 4) + 1, jnp.int32)
        cond_128 = 0.0061147 + 1.02565 * jax.random.normal(jax.random.fold_in(_rk, 11), (32, 128), jnp.float32)
        fside_S_0 = -0.022604 + 0.987366 * jax.random.normal(jax.random.fold_in(_rk, 12), (64,), jnp.float32)
        return (x, cond_128, fside_S_0)
    x, cond_128, fside_S_0 = _rec_inputs()

    def _L0_cond_setup():
        import jax, jax.numpy as jnp
        import numpy as np
        K = 8
        T = 1.0
        D_EMBD = 128
        IN_C = 64
        OUT_C = 64
        BS = 32
        H = 1024
        HID = 128
        key = jax.random.key(seed)
        ks = jax.random.split(key, 10)
        s = lambda fan_in: 1.0 / np.sqrt(fan_in)
        return {'x': jax.random.normal(ks[0], (BS, IN_C, H), dtype=jnp.float32), 'embedding': jax.random.normal(ks[1], (BS, D_EMBD), dtype=jnp.float32), 'W0': jax.random.normal(ks[2], (D_EMBD, HID), dtype=jnp.float32) * s(D_EMBD), 'b0': jnp.zeros((HID,), dtype=jnp.float32), 'W1': jax.random.normal(ks[3], (HID, HID), dtype=jnp.float32) * s(HID), 'b1': jnp.zeros((HID,), dtype=jnp.float32), 'W2': jax.random.normal(ks[4], (HID, K), dtype=jnp.float32) * s(HID), 'b2': jnp.zeros((K,), dtype=jnp.float32), 'weight': jax.random.normal(ks[5], (K, OUT_C, IN_C, 1), dtype=jnp.float32) * s(IN_C), 'bias_k': jax.random.normal(ks[6], (K, OUT_C), dtype=jnp.float32) * 0.1}
    _L0_cond_all = _L0_cond_setup()
    _L0_cond_in = {k: v for k, v in _L0_cond_all.items() if k in ('W0', 'b0', 'W1', 'b1', 'W2', 'b2', 'weight', 'bias_k')}
    del _L0_cond_all

    def _L0_ffn_setup():
        import jax, jax.numpy as jnp
        import numpy as np

        @jax.custom_vjp
        def ste_sign(w):
            return jnp.sign(w)

        def _ste_fwd(w):
            return (jnp.sign(w), w)

        def _ste_bwd(w, g):
            mask = ((w > -1) & (w < 1)).astype(g.dtype)
            return (g * mask,)
        ste_sign.defvjp(_ste_fwd, _ste_bwd)
        key = jax.random.key(seed)
        k = jax.random.split(key, 6)
        B, S, H, O, E = (4, 512, 1024, 1024, 8)
        return {'x': jax.random.normal(k[0], (B, S, H), dtype=jnp.float32), 'weight': jax.random.normal(k[1], (O, H), dtype=jnp.float32) * 0.02, 'bias': jax.random.normal(k[2], (O,), dtype=jnp.float32) * 0.02, 'gate_w': jax.random.normal(k[3], (E, H), dtype=jnp.float32) * 0.02, 'in_channel_scale': jax.random.normal(k[4], (E, H), dtype=jnp.float32), 'out_channel_scale': jax.random.normal(k[5], (E, O), dtype=jnp.float32)}
    _L0_ffn_all = _L0_ffn_setup()
    _L0_ffn_in = {k: v for k, v in _L0_ffn_all.items() if k in ('weight', 'bias', 'gate_w', 'in_channel_scale', 'out_channel_scale')}
    del _L0_ffn_all

    def _L1_cond_setup():
        import jax, jax.numpy as jnp
        import numpy as np
        from jax import lax
        N, C_IN, L = (32, 64, 1024)
        C_OUT, K, GROUPS = (64, 9, 4)
        C_DIM, PAD, STRIDE = (128, 4, 1)
        key = jax.random.key(seed)
        k1, k2, k3, k4, k5 = jax.random.split(key, 5)
        x = jax.random.normal(k1, (N, C_IN, L), dtype=jnp.float32)
        c = jax.random.normal(k2, (N, C_DIM), dtype=jnp.float32)
        weight = jax.random.normal(k3, (C_OUT, C_IN // GROUPS, K), dtype=jnp.float32)
        c_weight = jax.random.normal(k4, (C_OUT, C_DIM), dtype=jnp.float32)
        bias = jax.random.normal(k5, (C_OUT,), dtype=jnp.float32)
        return {'x': x, 'c': c, 'weight': weight, 'c_weight': c_weight, 'bias': bias}
    _L1_cond_all = _L1_cond_setup()
    _L1_cond_in = {k: v for k, v in _L1_cond_all.items() if k in ('weight', 'c_weight')}
    del _L1_cond_all

    def _L1_ffn_setup():
        import jax, jax.numpy as jnp
        import numpy as np
        import math
        E, DK, R = (8, 32, 16)
        SCALING = 16.0 / 16.0
        key = jax.random.key(seed)
        ks = jax.random.split(key, 7)
        Bt, S, Din, Dout = (4, 512, 1024, 1024)
        x = jax.random.normal(ks[0], (Bt, S, Din), jnp.float32)
        W = jax.random.normal(ks[1], (Dout, Din), jnp.float32) * 0.02
        b = jnp.zeros((Dout,), jnp.float32)
        Wq = jax.random.normal(ks[2], (E * DK, Din), jnp.float32) * 0.02
        Wk = jax.random.normal(ks[3], (E * DK, Din), jnp.float32) * 0.02
        A = jax.random.normal(ks[4], (E, R, Din), jnp.float32) * 0.02
        Bm = jax.random.normal(ks[5], (E, Dout, R), jnp.float32) * 0.02
        return {'x': x, 'W': W, 'b': b, 'Wq': Wq, 'Wk': Wk, 'A': A, 'Bm': Bm}
    _L1_ffn_all = _L1_ffn_setup()
    _L1_ffn_in = {k: v for k, v in _L1_ffn_all.items() if k in ('W', 'b', 'Wq', 'Wk', 'A', 'Bm')}
    del _L1_ffn_all
    return {'x': x, 'cond_128': cond_128, 'fside_S_0': fside_S_0, 'L0_cond_W0': _L0_cond_in['W0'], 'L0_cond_b0': _L0_cond_in['b0'], 'L0_cond_W1': _L0_cond_in['W1'], 'L0_cond_b1': _L0_cond_in['b1'], 'L0_cond_W2': _L0_cond_in['W2'], 'L0_cond_b2': _L0_cond_in['b2'], 'L0_cond_weight': _L0_cond_in['weight'], 'L0_cond_bias_k': _L0_cond_in['bias_k'], 'L0_ffn_weight': _L0_ffn_in['weight'], 'L0_ffn_bias': _L0_ffn_in['bias'], 'L0_ffn_gate_w': _L0_ffn_in['gate_w'], 'L0_ffn_in_channel_scale': _L0_ffn_in['in_channel_scale'], 'L0_ffn_out_channel_scale': _L0_ffn_in['out_channel_scale'], 'L1_cond_weight': _L1_cond_in['weight'], 'L1_cond_c_weight': _L1_cond_in['c_weight'], 'L1_ffn_W': _L1_ffn_in['W'], 'L1_ffn_b': _L1_ffn_in['b'], 'L1_ffn_Wq': _L1_ffn_in['Wq'], 'L1_ffn_Wk': _L1_ffn_in['Wk'], 'L1_ffn_A': _L1_ffn_in['A'], 'L1_ffn_Bm': _L1_ffn_in['Bm']}

def reference(x, cond_128, fside_S_0, L0_cond_W0, L0_cond_b0, L0_cond_W1, L0_cond_b1, L0_cond_W2, L0_cond_b2, L0_cond_weight, L0_cond_bias_k, L0_ffn_weight, L0_ffn_bias, L0_ffn_gate_w, L0_ffn_in_channel_scale, L0_ffn_out_channel_scale, L1_cond_weight, L1_cond_c_weight, L1_ffn_W, L1_ffn_b, L1_ffn_Wq, L1_ffn_Wk, L1_ffn_A, L1_ffn_Bm):
    import jax
    import jax.numpy as jnp

    def _L0_cond_ref(x, embedding, W0, b0, W1, b1, W2, b2, weight, bias_k):
        import jax, jax.numpy as jnp
        import numpy as np
        K = 8
        T = 1.0
        D_EMBD = 128
        IN_C = 64
        OUT_C = 64
        BS = 32
        H = 1024
        HID = 128
        h = jax.nn.gelu(embedding @ W0 + b0, approximate=False)
        h = jax.nn.gelu(h @ W1 + b1, approximate=False)
        att = jax.nn.softmax((h @ W2 + b2) / T, axis=-1)
        agg_w = jnp.einsum('bk,koi->boi', att, weight[..., 0])
        agg_b = att @ bias_k
        out = jnp.einsum('boi,bih->boh', agg_w, x) + agg_b[:, :, None]
        return out

    def _L0_ffn_ref(x, weight, bias, gate_w, in_channel_scale, out_channel_scale):
        import jax, jax.numpy as jnp
        import numpy as np

        @jax.custom_vjp
        def ste_sign(w):
            return jnp.sign(w)

        def _ste_fwd(w):
            return (jnp.sign(w), w)

        def _ste_bwd(w, g):
            mask = ((w > -1) & (w < 1)).astype(g.dtype)
            return (g * mask,)
        ste_sign.defvjp(_ste_fwd, _ste_bwd)
        B, S, H = x.shape
        xf = x.reshape(-1, H)
        router_logits = xf @ gate_w.T
        routing = jax.nn.softmax(router_logits.astype(jnp.float32), axis=1).astype(x.dtype)
        in_scale = routing @ in_channel_scale
        out_scale = routing @ out_channel_scale
        wb = ste_sign(weight)
        out = xf * in_scale @ wb.T * out_scale + bias
        return out.reshape(B, S, -1)

    def _L1_cond_ref(x, c, weight, c_weight, bias):
        import jax, jax.numpy as jnp
        import numpy as np
        from jax import lax
        N, C_IN, L = (32, 64, 1024)
        C_OUT, K, GROUPS = (64, 9, 4)
        C_DIM, PAD, STRIDE = (128, 4, 1)
        out = lax.conv_general_dilated(x, weight, window_strides=(STRIDE,), padding=[(PAD, PAD)], dimension_numbers=('NCH', 'OIH', 'NCH'), feature_group_count=GROUPS)
        ctx = jnp.einsum('nd,od->no', c, c_weight)
        out = out + ctx[:, :, None] + bias[None, :, None]
        return out

    def _L1_ffn_ref(x, W, b, Wq, Wk, A, Bm):
        import jax, jax.numpy as jnp
        import numpy as np
        import math
        E, DK, R = (8, 32, 16)
        SCALING = 16.0 / 16.0
        Bt, S, Din = x.shape
        result = jnp.einsum('bsi,oi->bso', x, W) + b
        q = jnp.einsum('bsi,ni->bsn', x, Wq).reshape(Bt, S, E, DK)
        k = jnp.einsum('bsi,ni->bsn', x, Wk).reshape(Bt, S, E, DK)
        scores = jnp.einsum('bsed,bsed->bse', q, k) / math.sqrt(DK)
        w = jax.nn.softmax(scores, axis=-1)
        h = jnp.einsum('bsi,eri->bser', x, A)
        combined = jnp.einsum('bse,bser,eor->bso', w, h, Bm) * SCALING
        return result + combined
    x = x + _L0_ffn_ref(_L0_cond_ref(x, cond_128, L0_cond_W0, L0_cond_b0, L0_cond_W1, L0_cond_b1, L0_cond_W2, L0_cond_b2, L0_cond_weight, L0_cond_bias_k), L0_ffn_weight, L0_ffn_bias, L0_ffn_gate_w, L0_ffn_in_channel_scale, L0_ffn_out_channel_scale)
    x = x + _L1_ffn_ref(_L1_cond_ref(x, cond_128, L1_cond_weight, L1_cond_c_weight, fside_S_0), L1_ffn_W, L1_ffn_b, L1_ffn_Wq, L1_ffn_Wk, L1_ffn_A, L1_ffn_Bm)
    return x

_drawn_inputs = setup_inputs


def setup_inputs(seed=0):
    import zlib

    import numpy as np

    out = dict(_drawn_inputs(seed))
    spreads = {'L0_cond_b0': (0.0, 0.1),
     'L0_cond_b1': (0.0, 0.1),
     'L0_cond_b2': (0.0, 0.1),
     'L1_ffn_b': (0.0, 0.8)}
    factors = {'L0_ffn_bias': 4.289}
    for name, (base, spread) in spreads.items():
        noise = np.random.default_rng([zlib.crc32(name.encode()), seed]).standard_normal(out[name].shape)
        drawn = base * np.exp(spread * noise) if base else spread * noise
        out[name] = jnp.asarray(drawn.astype(out[name].dtype))
    for name, factor in factors.items():
        out[name] = (out[name] * factor).astype(out[name].dtype)
    return out
```

```python
from contextlib import ExitStack

import concourse.bass as bass
from concourse import mybir

F32 = mybir.dt.float32
F32R = mybir.dt.float32r
ALU = mybir.AluOpType
ACT = mybir.ActivationFunctionType
AX = mybir.AxisListType

P = 128
B, S, H = 32, 64, 1024
TILES = B * S // P
PAIRS = TILES // 2
L8 = H // P
HALF = 512
E = 8
K8 = 8
R = 16
DK = 32
GROUPS, CG, TAPS = 4, 16, 9
NBG = 2 * GROUPS
NB = P + 1
NQK = 2 * E * DK
NA = E * R
NW = NQK + NA + HALF
C_W0, C_W1, C_W2 = 0, 128, 256
C_CW, C_CT, C_B0, C_B1 = 264, 328, 360, 361
C_GATE, C_ID = 362, 426
C_END = 554
R_B2, R_FS, R_BK, R_LO, R_SG = 0, 8, 72, 136, 137
R_END = 138


def adaln_ffn_kernel(nc, x, consts, rows, mix, wsign, scales, bias0, toep, wearly, wlate, bm, bias1, out):
    x1_dram = nc.dram_tensor("x1_scratch", (TILES * P, H), F32, kind="Internal").ap()
    rows_dram = nc.dram_tensor("token_rows_scratch", (2, B, S), F32, kind="Internal").ap()
    aggb_row = rows_dram[0:1].rearrange("a b s -> a (b s)")
    ctx_row = rows_dram[1:2].rearrange("a b s -> a (b s)")

    ctx = ExitStack()
    with ctx:
        def sb(name, shape, dt=F32):
            return ctx.enter_context(nc.sbuf_tensor(name, shape, dt))

        def sem(name):
            return ctx.enter_context(nc.semaphore(name))

        def sems(name):
            return [sem(f"{name}{p}") for p in range(2)]

        cst = sb("cst", [P, C_END])
        rws = sb("rws", [64, R_END])
        late = sb("late", [P, 2 * L8 * HALF], F32R)
        early = sb("early", [P, 2, L8, NW], F32R)
        lora = sb("lora", [P, 2, H], F32R)
        band = sb("band", [P, 2, 2 * GROUPS, P], F32R)
        stage = sb("stage", [P, 2, NW])
        scale_w = sb("scale_w", [64, H], F32R)
        parts = sb("parts", [P, 2, 2, L8, P], F32R)
        work = sb("work", [P, 4, H])
        xs = sb("xs", [P, 2, H])
        shared = sb("shared", [P, 2 * NBG * NB])
        taps = sb("taps", [P, 2, NBG, NB], F32R)
        bias_bc = sb("bias_bc", [P, H])
        row_bc = sb("row_bc", [P, 2, P])
        routing = sb("routing", [P, 4, 4, E], F32R)
        routing_t = sb("routing_t", [64, P], F32R)
        gate = sb("gate", [P, 64])
        qk = sb("qk", [P, 2, NQK // 2])
        wh = sb("wh", [P, NA])
        wh_t = sb("wh_t", [P, 2, P], F32R)
        hid = sb("hid", [P, 2, B])
        att = sb("att", [B, 64])
        att_t = sb("att_t", [K8, B])
        tok_rows = sb("tok_rows", [B, 2, S])

        signs = late[:, :].rearrange("p (c n) -> p c n", c=L8)
        wlate_s = late[:, :].rearrange("p (a c n) -> p a c n", a=2, c=L8)
        y_t = work[:, 0, :].rearrange("p (c t) -> p c t", c=L8)
        os_sb = work[:, 1, :]
        resid = work[:, 2:4, :]
        mix_w = work[0:K8, :, :].rearrange("k a n -> k (a n)").rearrange("k (o i) -> k o i", o=S)
        agg = shared[:, 0:B * S]
        agg_bo = agg.rearrange("p (b o) -> p b o", b=B)
        raw = shared[:, :].rearrange("p (a n r) -> p a n r", a=2, n=NBG)
        ident = cst[:, C_ID:C_ID + P]

        bank = [ctx.enter_context(nc.psum_tensor(f"bank{k}", [P, HALF], F32)) for k in range(8)]

        consts_loaded = sem("consts_loaded")
        rows_loaded = sem("rows_loaded")
        mix_loaded = sem("mix_loaded")
        scales_loaded = sem("scales_loaded")
        bias0_loaded = sem("bias0_loaded")
        bias1_loaded = sem("bias1_loaded")
        x_loaded = sems("x_loaded")
        aggb_loaded = sems("aggb_loaded")
        ctx_loaded = sems("ctx_loaded")
        stage_loaded = sems("stage_loaded")
        stage_hi = sems("stage_hi")
        stage_lo = sems("stage_lo")
        rows_stored = sem("rows_stored")

        mlp_done = sem("mlp_done")
        mlp_act = sem("mlp_act")
        ctx_done = sem("ctx_done")
        att_step = sem("att_step")
        att_exp = sem("att_exp")
        att_turned = sem("att_turned")
        att_t_ready = sem("att_t_ready")
        aggb_done = sem("aggb_done")
        tok_rows_ready = sem("tok_rows_ready")
        agg_zeroed = sem("agg_zeroed")
        agg_done = sem("agg_done")
        agg_ready = sem("agg_ready")
        scale_hi = sem("scale_hi")
        scale_signed = sem("scale_signed")
        scale_ready = sem("scale_ready")

        y_done = sem("y_done")
        y_biased = sem("y_biased")
        logits_done = sem("logits_done")
        gate_max = sem("gate_max")
        gate_exp = sem("gate_exp")
        gate_rcp = sem("gate_rcp")
        gate_prob = sem("gate_prob")
        routing_zeroed = sem("routing_zeroed")
        routing_hi = sem("routing_hi")
        routing_ready = sem("routing_ready")
        routing_turned = sem("routing_turned")
        routing_copied = sem("routing_copied")
        in_scale_done = sem("in_scale_done")
        out_scale_done = sem("out_scale_done")
        u_ready = sem("u_ready")
        u_hi = sem("u_hi")
        u_lo = sem("u_lo")
        ffn0_done = sem("ffn0_done")
        out_scale_ready = sem("out_scale_ready")
        scaled = sem("scaled")
        xb_ready = sem("xb_ready")
        x1_ready = sem("x1_ready")
        x1_stored = sems("x1_stored")

        pads_zeroed = sem("pads_zeroed")
        raw_loaded = sems("raw_loaded")
        taps_hi = sem("taps_hi")
        taps_lo = sem("taps_lo")
        conv_done = sem("conv_done")
        z_biased = sem("z_biased")
        z_hi = sem("z_hi")
        z_lo = sem("z_lo")
        qk_done = sem("qk_done")
        k_copied = sem("k_copied")
        qk_mult = sem("qk_mult")
        scores_ready = sem("scores_ready")
        score_max = sem("score_max")
        score_exp = sem("score_exp")
        score_rcp = sem("score_rcp")
        weights_ready = sem("weights_ready")
        lora_done = sem("lora_done")
        wh_ready = sem("wh_ready")
        wh_turned = sem("wh_turned")
        wh_hi = sem("wh_hi")
        wh_lo = sem("wh_lo")
        ffn1_done = sem("ffn1_done")
        resid_loaded = sems("resid_loaded")
        resid_ready = sem("resid_ready")
        out_ready = sem("out_ready")
        out_stored = sems("out_stored")

        block = ctx.enter_context(nc.Block())

        def tile_rows(dram, t):
            return dram[bass.ds(t * P, P), :]

        @block.sync
        def _(sp):
            def load_x(i, p):
                sp.dma_start(xs[:, p, :], tile_rows(x, 2 * i + p)).then_inc(x_loaded[p], 16)

            def load_row(row, i, p, loaded):
                src = row[0:1, bass.ds((2 * i + p) * P, P)]
                sp.dma_start(row_bc[:, p, :], src.broadcast_to([P, P])).then_inc(loaded[p], 16)

            def load_stage(p, src, n):
                sp.dma_start(stage[:, p, 0:n], src).then_inc(stage_loaded[p], 16)

            sp.dma_start(cst[:, :], consts).then_inc(consts_loaded, 16)
            sp.dma_start(rws[:, :], rows).then_inc(rows_loaded, 16)
            sp.dma_start(work[0:K8, :, :].rearrange("k a n -> k (a n)"), mix).then_inc(mix_loaded, 16)
            sp.dma_start(bias_bc[0:64, :], scales).then_inc(scales_loaded, 16)
            load_x(0, 0)
            load_x(0, 1)
            for c in range(2):
                load_stage(c, wsign[:, c, :], H)
            sp.wait_ge(scale_ready, 1)
            sp.dma_start(bias_bc[:, :], bias0.broadcast_to([P, H])).then_inc(bias0_loaded, 16)
            sp.wait_ge(tok_rows_ready, 2)
            sp.dma_start(rows_dram.rearrange("a b s -> b a s"), tok_rows[:, :, :]).then_inc(rows_stored, 16)
            sp.wait_ge(rows_stored, 16)
            load_row(aggb_row, 0, 0, aggb_loaded)
            load_row(aggb_row, 0, 1, aggb_loaded)
            sp.wait_ge(stage_hi[0], 4)
            load_stage(0, wearly[:, 0, :], NW)
            sp.wait_ge(stage_hi[1], 4)
            load_stage(1, toep, H)

            def store_x1(i, p, both):
                sp.wait_ge(x1_ready, both)
                sp.dma_start(tile_rows(x1_dram, 2 * i + p), resid[:, p, :]).then_inc(x1_stored[p], 16)

            def step0(i, p):
                both = 4 * i + 2 * p + 2
                sp.wait_ge(xb_ready, both)
                sp.wait_ge(y_biased, both)
                load_x(i + 1, p)
                load_row(aggb_row, i + 1, p, aggb_loaded)
                store_x1(i, p, both)

            sp.wait_ge(stage_hi[1], 5)
            sp.wait_ge(stage_lo[1], 1)
            load_stage(1, bm, H)
            with sp.Fori(0, PAIRS - 1) as i:
                step0(i, 0)
                sp.wait_ge(stage_hi[0], i + 5)
                sp.wait_ge(stage_lo[0], i + 1)
                load_stage(0, wearly[:, bass.ds(i + 1, 1), :].rearrange("p a n -> p (a n)"), NW)
                step0(i, 1)

            last = PAIRS - 1
            for p in range(2):
                sp.wait_ge(y_biased, 4 * last + 2 * p + 2)
                load_row(ctx_row, 0, p, ctx_loaded)

            def load_raw(i, p):
                sp.wait_ge(x1_stored[p], 16 * (i + 1))
                src = tile_rows(x1_dram, 2 * i + p).rearrange("(n c) (l q) -> l c n q", c=CG, l=L8)
                half = L8 // 2
                for lo in range(2):
                    for l in range(half):
                        part = (lo * half + l) * CG
                        at = 1 - lo
                        sp.dma_start(raw[part:part + CG, p, :, at:at + P],
                                     src[(1 - lo) * half + l]).then_inc(raw_loaded[p], 16)

            sp.wait_ge(pads_zeroed, 2)
            load_raw(0, 0)
            load_raw(0, 1)
            sp.wait_ge(xb_ready, 2 * TILES)
            sp.dma_start(bias_bc[:, :], bias1.broadcast_to([P, H])).then_inc(bias1_loaded, 16)
            store_x1(last, 0, 4 * last + 2)
            for p in range(2):
                sp.wait_ge(stage_hi[p], (12, 6)[p])
                sp.wait_ge(stage_lo[p], (8, 2)[p])
                load_stage(p, wlate[:, p, :], HALF)
            store_x1(last, 1, 4 * last + 4)

            def load_resid(i, p):
                sp.dma_start(resid[:, p, :], tile_rows(x1_dram, 2 * i + p)).then_inc(resid_loaded[p], 16)

            for p in range(2):
                sp.wait_ge(x1_stored[p], 16 * PAIRS)
                load_resid(0, p)
            for c in range(2, L8):
                p = c % 2
                sp.wait_ge(stage_hi[p], (12, 6)[p] + c // 2)
                sp.wait_ge(stage_lo[p], (8, 2)[p] + c // 2)
                load_stage(p, wlate[:, c, :], HALF)

            def store_out(i, p, both):
                sp.wait_ge(out_ready, both)
                sp.dma_start(tile_rows(out, 2 * i + p), resid[:, p, :]).then_inc(out_stored[p], 16)

            with sp.Fori(0, PAIRS - 1) as i:
                for p in range(2):
                    both = 4 * i + 2 * p + 2
                    sp.wait_ge(taps_lo, both)
                    sp.wait_ge(z_biased, both)
                    load_raw(i + 1, p)
                    load_row(ctx_row, i + 1, p, ctx_loaded)
                    store_out(i, p, both)
                    sp.wait_ge(out_stored[p], 16 * (i + 1))
                    load_resid(i + 1, p)
            store_out(last, 0, 4 * last + 2)
            store_out(last, 1, 4 * last + 4)
            for p in range(2):
                sp.wait_ge(out_stored[p], 16 * PAIRS)

        @block.tensor
        def _(pe):
            mm = nc.tensor.matmul
            pe.wait_ge(consts_loaded, 16)
            mm(bank[0][:, 0:B], cst[:, C_W0:C_W0 + P], cst[:, C_CT:C_CT + B], start=True, stop=True).then_inc(mlp_done, 1)
            mm(bank[1][0:B, 0:S], cst[:, C_CT:C_CT + B], cst[:, C_CW:C_CW + S], start=True, stop=True).then_inc(ctx_done, 1)
            pe.wait_ge(mlp_act, 1)
            mm(bank[0][:, B:2 * B], cst[:, C_W1:C_W1 + P], hid[:, 0, :], start=True, stop=True).then_inc(mlp_done, 1)
            pe.wait_ge(mlp_act, 2)
            mm(bank[2][0:B, 0:K8], hid[:, 1, :], cst[:, C_W2:C_W2 + K8], start=True, stop=True).then_inc(mlp_done, 1)
            pe.wait_ge(att_step, 5)
            nc.tensor.transpose(bank[3][0:K8, 0:B], att[:, 32:32 + K8], ident[0:B, 0:B]).then_inc(att_turned, 1)
            pe.wait_ge(att_t_ready, 1)
            pe.wait_ge(rows_loaded, 16)
            mm(bank[0][0:B, 0:S], att_t[:, :], rws[0:K8, R_BK:R_BK + S], start=True, stop=True).then_inc(aggb_done, 1)
            pe.wait_ge(mix_loaded, 16)
            for o in range(S):
                k, at = 4 + o // 16, (o % 16) * B
                for h in range(2):
                    last = mm(bank[k][64 * h:64 * h + 64, at:at + B], mix_w[:, o, :], att_t[:, :],
                              start=True, stop=True)
                if o % 16 == 15:
                    last.then_inc(agg_done, 1)

            def product_y(i, p):
                pe.wait_ge(x_loaded[p], 16 * (i + 1))
                for h in range(2):
                    for c in range(4):
                        at = (4 * h + c) * P
                        last = mm(bank[h][:, c * P:(c + 1) * P], xs[:, p, at:at + P],
                                  agg[:, bass.ds((2 * i + p) * P, P)], start=True, stop=True)
                last.then_inc(y_done, 1)

            def product_logits(i, p):
                pe.wait_ge(y_biased, 4 * i + 2 * p + 2)
                for c in range(L8):
                    last = mm(bank[2][:, 0:E], y_t[:, c, :], cst[:, C_GATE + c * E:C_GATE + (c + 1) * E],
                              start=(c == 0), stop=(c == L8 - 1))
                last.then_inc(logits_done, 1)

            def product_scales(i, p):
                pe.wait_ge(routing_ready, 2 * i + p + 1)
                nc.tensor.transpose(bank[3][:, 0:P], routing[:, :, :, :].bitcast(F32).rearrange("p a b e -> p (a b e)"),
                                    ident).then_inc(routing_turned, 1)
                pe.wait_ge(routing_copied, 2 * i + p + 1)
                for h in range(2):
                    for c in range(4):
                        at = (4 * h + c) * P
                        last = mm(bank[2 + h][:, c * P:(c + 1) * P], scale_w[0:32, at:at + P], routing_t[0:32, :],
                                  start=True, stop=True)
                    last.then_inc(in_scale_done, 1)
                for h in range(2):
                    mm(bank[6 + h][:, :], routing_t[32:64, :], scale_w[32:64, h * HALF:(h + 1) * HALF],
                       start=True, stop=True).then_inc(out_scale_done, 1)

            def product_ffn0(p, h, blocks):
                for c in blocks:
                    for a in range(2):
                        last = mm(bank[4 + h][:, :], parts[:, p, a, c, :], signs[:, c, h * HALF:(h + 1) * HALF],
                                  start=(c == 0 and a == 0), stop=(c == L8 - 1 and a == 1))
                if blocks[-1] == L8 - 1:
                    last.then_inc(ffn0_done, 1)

            first, second = range(L8 // 2), range(L8 // 2, L8)

            def ffn0_a(i, p, first_tile=False):
                pe.wait_ge(u_hi, 4 * i + 2 * p + 2)
                pe.wait_ge(u_lo, 4 * i + 2 * p + 2)
                if not first_tile:
                    pe.wait_ge(scaled, 4 * i + 2 * p - 1)
                product_ffn0(p, 0, first)

            def ffn0_b(i, p):
                product_ffn0(p, 0, second)
                pe.wait_ge(scaled, 4 * i + 2 * p)
                product_ffn0(p, 1, first)

            pe.wait_ge(agg_ready, 8)
            product_y(0, 0)
            product_logits(0, 0)
            pe.wait_ge(scale_ready, 1)
            pe.wait_ge(routing_zeroed, 1)
            product_scales(0, 0)

            def period0(i, p, ni, q, first_tile=False):
                pe.wait_ge(y_biased, 4 * i + 2 * p + 2)
                product_y(ni, q)
                if first_tile:
                    for k in range(2):
                        pe.wait_ge(stage_hi[k], 4)
                ffn0_a(i, p, first_tile)
                pe.wait_ge(u_ready, 4 * i + 2 * p + 2)
                product_logits(ni, q)
                ffn0_b(i, p)
                pe.wait_ge(out_scale_ready, 4 * i + 2 * p + 2)
                product_scales(ni, q)
                product_ffn0(p, 1, second)

            period0(0, 0, 0, 1, True)
            period0(0, 1, 1, 0)
            with pe.Fori(1, PAIRS - 1) as i:
                period0(i, 0, i, 1)
                period0(i, 1, i + 1, 0)
            last_i = PAIRS - 1
            period0(last_i, 0, last_i, 1)

            def product_conv(i, p):
                pe.wait_ge(taps_hi, 2 * i + p + 1)
                pe.wait_ge(taps_lo, 4 * i + 2 * p + 2)
                for n in range(NBG):
                    dst = bank[n // 4][:, (n % 4) * P:(n % 4 + 1) * P]
                    k = 0
                    for s in range(2):
                        for a, b in ((0, 0), (0, 1), (1, 0)):
                            last = mm(dst, taps[:, a, n, s:s + P], band[:, b, s * GROUPS + n % 4, :],
                                      start=(k == 0), stop=(k == 5))
                            k += 1
                    if n % 4 == 3:
                        last.then_inc(conv_done, 1)

            ffn0_a(last_i, 1)
            ffn0_b(last_i, 1)
            pe.wait_ge(y_biased, 2 * TILES)
            pe.wait_ge(stage_hi[1], 5)
            pe.wait_ge(stage_lo[1], 1)
            product_conv(0, 0)
            product_ffn0(1, 1, second)

            def split_product(dst, lhs, rhs, blocks, start, stop):
                n = len(blocks)
                for j, c in enumerate(blocks):
                    for k, (a, b) in enumerate(((0, 0), (0, 1), (1, 0))):
                        last = mm(dst, lhs(a, c), rhs(b, c), start=(start and j == 0 and k == 0),
                                  stop=(stop and j == n - 1 and k == 2))
                return last

            blocks = list(range(L8))

            def period1(i, p, ni, q):
                zp = lambda a, c: parts[:, p, a, c, :]
                pe.wait_ge(z_hi, 4 * i + 2 * p + 2)
                pe.wait_ge(z_lo, 4 * i + 2 * p + 2)
                split_product(bank[2][:, :], zp, lambda b, c: early[:, b, c, 0:NQK], blocks, True, True).then_inc(qk_done, 1)
                split_product(bank[3][:, 0:NA], zp, lambda b, c: early[:, b, c, NQK:NQK + NA], blocks, True, True)\
                    .then_inc(lora_done, 1)
                if ni is not None:
                    product_conv(ni, q)
                o0, o1 = bank[4 + 2 * p], bank[5 + 2 * p]
                split_product(o0[:, :], zp, lambda b, c: early[:, b, c, NQK + NA:NW], blocks, True, False)
                pe.wait_ge(wh_ready, 2 * i + p + 1)
                nc.tensor.transpose(bank[3][:, 0:P], wh[:, :], ident).then_inc(wh_turned, 1)
                return zp, o0, o1

            def period1_end(i, p, zp, o0, o1):
                split_product(o1[:, :], zp, lambda b, c: wlate_s[:, b, c, :], blocks, True, False)
                pe.wait_ge(wh_hi, 2 * i + p + 1)
                pe.wait_ge(wh_lo, 2 * i + p + 1)
                for h, o in enumerate((o0, o1)):
                    split_product(o[:, :], lambda a, c: wh_t[:, a, :], lambda b, c: lora[:, b, h * HALF:(h + 1) * HALF],
                                  [0], False, True).then_inc(ffn1_done, 1)

            pe.wait_ge(stage_hi[0], 12)
            pe.wait_ge(stage_lo[0], 8)
            pe.wait_ge(stage_hi[1], 6)
            pe.wait_ge(stage_lo[1], 2)
            pe.wait_ge(z_biased, 2)
            pe.wait_ge(scaled, 2 * TILES)
            pe.wait_ge(u_ready, 2 * TILES)
            pe.wait_ge(out_scale_ready, 2 * TILES)
            rest = period1(0, 0, 0, 1)
            for p in range(2):
                pe.wait_ge(stage_hi[p], (12, 6)[p] + 4)
                pe.wait_ge(stage_lo[p], (8, 2)[p] + 4)
            period1_end(0, 0, *rest)

            def gates(i, p):
                pe.wait_ge(qk_mult, 2 * i + p)
                pe.wait_ge(z_biased, 4 * i + 2 * p + 2)

            gates(0, 1)
            period1_end(0, 1, *period1(0, 1, 1, 0))
            with pe.Fori(1, PAIRS - 1) as i:
                for p in range(2):
                    gates(i, p)
                    pe.wait_ge(out_ready, 4 * i + 2 * p - 2)
                    period1_end(i, p, *period1(i, p, i + p, 1 - p))
            gates(last_i, 0)
            pe.wait_ge(out_ready, 4 * last_i - 2)
            period1_end(last_i, 0, *period1(last_i, 0, last_i, 1))
            gates(last_i, 1)
            pe.wait_ge(out_ready, 4 * last_i)
            period1_end(last_i, 1, *period1(last_i, 1, None, None))

        @block.scalar
        def _(act):
            do = nc.scalar.activation
            for k in range(2):
                act.wait_ge(mlp_done, k + 1)
                do(hid[:, k, :], bank[0][:, k * B:(k + 1) * B], ACT.Gelu,
                   bias=cst[:, C_B0 + k:C_B0 + k + 1]).then_inc(mlp_act, 1)
            act.wait_ge(att_step, 2)
            do(att[:, 16:16 + K8], att[:, 0:K8], ACT.Exp, bias=att[:, 8:9], accum_out=att[:, 9:10]).then_inc(att_exp, 1)
            act.wait_ge(scales_loaded, 16)
            do(scale_w[:, :], bias_bc[0:64, :], ACT.Copy).then_inc(scale_hi, 1)

            def sign_chunk(c):
                p = c % 2
                act.wait_ge(stage_loaded[p], 16 * (c // 2 + 1))
                do(signs[:, c, :], stage[:, p, 0:H], ACT.Sign).then_inc(stage_hi[p], 1)
                if c + 2 < L8:
                    act.wait_ge(stage_hi[p], c // 2 + 1)
                    act.dma_start(stage[:, p, 0:H], wsign[:, c + 2, :]).then_inc(stage_loaded[p], 16)

            for c in range(2):
                sign_chunk(c)
            for k in range(4):
                act.wait_ge(agg_zeroed, 1)
                act.wait_ge(agg_done, k + 1)
                src = bank[4 + k][64:128, :].rearrange("p (o b) -> p b o", b=B)
                do(agg_bo[64:128, 1::2, 16 * k:16 * k + 16], src[:, 1::2, :], ACT.Copy).then_inc(agg_ready, 1)
            for c in range(2, L8):
                sign_chunk(c)

            def gate_exps(i, p):
                act.wait_ge(gate_max, 2 * i + p + 1)
                do(gate[:, 8:16], bank[2][:, 0:E], ACT.Exp, bias=gate[:, 0:1], accum_out=gate[:, 1:2]).then_inc(gate_exp, 1)

            def copy_routing(i, p):
                act.wait_ge(routing_turned, 2 * i + p + 1)
                do(routing_t[:, :], bank[3][0:64, 0:P], ACT.Copy).then_inc(routing_copied, 1)

            def round_parts(i, p, ready, done, cols):
                for h in range(2):
                    act.wait_ge(ready, 4 * i + 2 * p + h + 1)
                    do(cols(parts[:, p, 0], h), cols(y_t, h), ACT.Copy).then_inc(done, 1)

            by_block = lambda a, h: a[:, 4 * h:4 * h + 4, :]
            by_token = lambda a, h: a[:, :, 64 * h:64 * h + 64]

            def copy_out_scale(i, p, reused):
                for h in range(2):
                    act.wait_ge(out_scale_done, 4 * i + 2 * p + h + 1)
                    if reused:
                        act.wait_ge(x1_ready, 4 * i + 2 * p - 1 + h)
                    do(os_sb[:, h * HALF:(h + 1) * HALF], bank[6 + h][:, :], ACT.Copy).then_inc(out_scale_ready, 1)

            def round_stage(p, n, loaded, dst):
                act.wait_ge(stage_loaded[p], loaded)
                do(dst, stage[:, p, 0:n], ACT.Copy).then_inc(stage_hi[p], 1)

            def tile0(i, p, reused=True, fresh=False):
                gate_exps(i, p)
                copy_routing(i, p)
                if not fresh:
                    act.wait_ge(ffn0_done, 4 * i + 2 * p - 2)
                round_parts(i, p, u_ready, u_hi, by_block)
                copy_out_scale(i, p, reused)

            tile0(0, 0, False, True)
            round_stage(1, H, 16 * 5, band[:, 0, :, :].rearrange("p a n -> p (a n)"))
            tile0(0, 1, True, True)
            with act.Fori(0, PAIRS - 1) as i:
                round_stage(0, NW, (i + 5) * 16, early[:, 0, bass.ds(i, 1), :].rearrange("p a n -> p (a n)"))
                tile0(i + 1, 0)
                tile0(i + 1, 1)
            def round_taps(i, p, first=False):
                act.wait_ge(raw_loaded[p], (i + 1) * (16 * L8))
                if not first:
                    act.wait_ge(conv_done, 4 * i + 2 * p)
                do(taps[:, 0, :, :], raw[:, p, :, :], ACT.Copy).then_inc(taps_hi, 1)

            round_taps(0, 0, True)
            round_stage(0, NW, 16 * 12, early[:, 0, L8 - 1, :])
            round_stage(1, H, 16 * 6, lora[:, 0, :])
            act.wait_ge(ffn0_done, 2 * TILES - 2)
            round_parts(0, 0, z_biased, z_hi, by_token)
            round_taps(0, 1)
            for c in range(L8):
                p = c % 2
                if c == 0:
                    act.wait_ge(ffn0_done, 2 * TILES)
                round_stage(p, HALF, 16 * ((12, 6)[p] + c // 2 + 1), wlate_s[:, 0, c, :])

            def period1(i, p, ni, q, nni):
                act.wait_ge(qk_done, 2 * i + p + 1)
                do(qk[:, 0, :], bank[2][:, NQK // 2:NQK], ACT.Copy).then_inc(k_copied, 1)
                act.wait_ge(score_max, 4 * i + 2 * p + 2)
                do(gate[:, 16:24], gate[:, 24:32], ACT.Exp, bias=gate[:, 2:3], scale=float(DK) ** -0.5,
                   accum_out=gate[:, 3:4]).then_inc(score_exp, 1)
                if ni is not None:
                    round_parts(ni, q, z_biased, z_hi, by_token)
                act.wait_ge(wh_turned, 2 * i + p + 1)
                do(wh_t[:, 0, :], bank[3][:, 0:P], ACT.Copy).then_inc(wh_hi, 1)
                if nni is not None:
                    round_taps(nni, p)

            with act.Fori(0, PAIRS - 1) as i:
                period1(i, 0, i, 1, i + 1)
                period1(i, 1, i + 1, 0, i + 1)
            last = PAIRS - 1
            period1(last, 0, last, 1, None)
            period1(last, 1, None, None, None)

        @block.vector
        def _(dve):
            v = nc.vector
            dve.wait_ge(rows_loaded, 16)
            dve.wait_ge(ctx_done, 1)
            v.tensor_tensor(tok_rows[:, 1, :], bank[1][0:B, 0:S], rws[0:B, R_FS:R_FS + S], ALU.add).then_inc(tok_rows_ready, 1)
            dve.wait_ge(mlp_done, 3)
            v.tensor_tensor(att[:, 0:K8], bank[2][0:B, 0:K8], rws[0:B, R_B2:R_B2 + K8], ALU.add).then_inc(att_step, 1)
            dve.wait_ge(att_step, 1)
            v.tensor_reduce(att[:, 8:9], att[:, 0:K8], AX.X, ALU.max, negate=True).then_inc(att_step, 1)
            dve.wait_ge(att_exp, 1)
            v.reciprocal(att[:, 10:11], att[:, 9:10]).then_inc(att_step, 1)
            dve.wait_ge(att_step, 3)
            v.tensor_scalar(att[:, 32:32 + K8], att[:, 16:16 + K8], att[:, 10:11], None, ALU.mult).then_inc(att_step, 2)
            dve.wait_ge(att_turned, 1)
            v.tensor_copy(att_t[:, :], bank[3][0:K8, 0:B]).then_inc(att_t_ready, 1)
            dve.wait_ge(aggb_done, 1)
            v.tensor_copy(tok_rows[:, 0, :], bank[0][0:B, 0:S]).then_inc(tok_rows_ready, 1)
            dve.wait_ge(scale_hi, 1)
            v.tensor_scalar(scale_w[:, :], scale_w[:, :].bitcast(F32), rws[:, R_SG:R_SG + 1], None,
                            ALU.mult).then_inc(scale_signed, 1)
            dve.wait_ge(scale_signed, 1)
            v.scalar_tensor_tensor(scale_w[:, :], bias_bc[0:64, :], rws[:, R_LO:R_LO + 1], scale_w[:, :].bitcast(F32),
                                   ALU.mult, ALU.add).then_inc(scale_ready, 1)
            v.memset(routing[:, 2:4, :, :].bitcast(F32), 0.0).then_inc(routing_zeroed, 1)
            dve.wait_ge(agg_zeroed, 1)
            for k in range(4):
                dve.wait_ge(agg_done, k + 1)
                src = bank[4 + k][0:64, :].rearrange("p (o b) -> p b o", b=B)
                v.tensor_copy(agg_bo[0:64, 0::2, 16 * k:16 * k + 16], src[:, 0::2, :]).then_inc(agg_ready, 1)


            def add_mix_bias(i, p, first_tile=False):
                dve.wait_ge(y_done, 2 * i + p + 1)
                dve.wait_ge(aggb_loaded[p], 16 * (i + 1))
                if not first_tile:
                    dve.wait_ge(u_lo, 4 * i + 2 * p)
                for h in range(2):
                    v.tensor_tensor(y_t[:, 4 * h:4 * h + 4, :], bank[h][:, :].rearrange("p (c t) -> p c t", c=4),
                                    row_bc[:, p:p + 1, :].broadcast_to([P, 4, P]), ALU.add).then_inc(y_biased, 1)

            def route(i, p):
                t1 = 2 * i + p + 1
                dve.wait_ge(logits_done, t1)
                v.tensor_reduce(gate[:, 0:1], bank[2][:, 0:E], AX.X, ALU.max, negate=True).then_inc(gate_max, 1)
                dve.wait_ge(gate_exp, t1)
                v.reciprocal(gate[:, 4:5], gate[:, 1:2]).then_inc(gate_rcp, 1)
                dve.wait_ge(gate_rcp, t1)
                dve.wait_ge(routing_ready, t1 - 1)
                v.tensor_scalar(gate[:, 32:40], gate[:, 8:16], gate[:, 4:5], None, ALU.mult).then_inc(gate_prob, 1)
                dve.wait_ge(gate_prob, t1)
                prob = gate[:, 32:40].rearrange("p (a b e) -> p a b e", a=1, b=1).broadcast_to([P, 2, 2, E])
                v.tensor_copy(routing[:, 0:2, 0:2, :], prob).then_inc(routing_hi, 1)
                dve.wait_ge(routing_hi, t1)
                v.tensor_tensor(routing[:, 0:2, 2:4, :], prob, routing[:, 0:2, 0:2, :].bitcast(F32),
                                ALU.subtract).then_inc(routing_ready, 1)

            def scale_in(i, p):
                for h in range(2):
                    dve.wait_ge(in_scale_done, 4 * i + 2 * p + h + 1)
                    y_h = y_t[:, 4 * h:4 * h + 4, :]
                    v.tensor_tensor(y_h, bank[2 + h][:, :].rearrange("p (c t) -> p c t", c=4), y_h,
                                    ALU.mult).then_inc(u_ready, 1)

            def take_rest(i, p, rounded, done, cols):
                for h in range(2):
                    dve.wait_ge(rounded, 4 * i + 2 * p + h + 1)
                    v.tensor_tensor(cols(parts[:, p, 1], h), cols(y_t, h), cols(parts[:, p, 0], h).bitcast(F32),
                                    ALU.subtract).then_inc(done, 1)

            def scale_out(i, p, h):
                dve.wait_ge(ffn0_done, 4 * i + 2 * p + h + 1)
                dve.wait_ge(out_scale_ready, 4 * i + 2 * p + h + 1)
                o = os_sb[:, h * HALF:(h + 1) * HALF]
                v.tensor_tensor(o, bank[4 + h][:, :], o, ALU.mult).then_inc(scaled, 1)

            by_block = lambda a, h: a[:, 4 * h:4 * h + 4, :]
            by_token = lambda a, h: a[:, :, 64 * h:64 * h + 64]

            def period0(i, p, ni, q, last_y=False):
                add_mix_bias(ni, q)
                if last_y:
                    v.memset(raw[0:64, :, :, 0:1], 0.0).then_inc(pads_zeroed, 1)
                    v.memset(raw[64:128, :, :, P:NB], 0.0).then_inc(pads_zeroed, 1)
                route(ni, q)
                scale_out(i, p, 0)
                scale_in(ni, q)
                take_rest(ni, q, u_hi, u_lo, by_block)
                scale_out(i, p, 1)

            add_mix_bias(0, 0, True)
            route(0, 0)
            scale_in(0, 0)
            take_rest(0, 0, u_hi, u_lo, by_block)
            with dve.Fori(0, PAIRS - 1) as i:
                period0(i, 0, i, 1)
                period0(i, 1, i + 1, 0)
            last = PAIRS - 1
            period0(last, 0, last, 1, True)
            scale_out(last, 1, 0)

            def add_context(i, p):
                dve.wait_ge(ctx_loaded[p], 16 * (i + 1))
                dve.wait_ge(z_lo, 4 * i + 2 * p)
                for h in range(2):
                    dve.wait_ge(conv_done, 4 * i + 2 * p + h + 1)
                    zt = y_t[:, :, 64 * h:64 * h + 64].rearrange("p l (n c) -> p n l c", c=CG)
                    add = row_bc[:, p:p + 1, 64 * h:64 * h + 64].rearrange("p l (n c) -> p n l c", c=CG)
                    v.tensor_tensor(zt, bank[h][:, :].rearrange("p (n l c) -> p n l c", n=4, l=L8),
                                    add.broadcast_to([P, 4, L8, CG]), ALU.add).then_inc(z_biased, 1)

            dve.wait_ge(u_lo, 2 * TILES)
            add_context(0, 0)
            take_rest(0, 0, z_hi, z_lo, by_token)
            scale_out(last, 1, 1)

            def period1(i, p, ni, q):
                t1 = 2 * i + p + 1
                dve.wait_ge(k_copied, t1)
                v.tensor_tensor(qk[:, 1, :], bank[2][:, 0:NQK // 2], qk[:, 0, :], ALU.mult).then_inc(qk_mult, 1)
                dve.wait_ge(qk_mult, t1)
                v.tensor_reduce(gate[:, 24:32], qk[:, 1, :].rearrange("p (e d) -> p e d", e=E), AX.X,
                                ALU.add).then_inc(scores_ready, 1)
                dve.wait_ge(scores_ready, t1)
                v.tensor_reduce(gate[:, 5:6], gate[:, 24:32], AX.X, ALU.max, negate=True).then_inc(score_max, 1)
                dve.wait_ge(score_max, 2 * t1 - 1)
                v.tensor_scalar(gate[:, 2:3], gate[:, 5:6], float(DK) ** -0.5, None, ALU.mult).then_inc(score_max, 1)
                dve.wait_ge(score_exp, t1)
                v.reciprocal(gate[:, 6:7], gate[:, 3:4]).then_inc(score_rcp, 1)
                dve.wait_ge(score_rcp, t1)
                dve.wait_ge(lora_done, t1)
                w = gate[:, 16:24].rearrange("p (e a) -> p e a", a=1).broadcast_to([P, E, R])
                v.scalar_tensor_tensor(wh[:, :].rearrange("p (e r) -> p e r", e=E), w, gate[:, 6:7],
                                       bank[3][:, 0:NA].rearrange("p (e r) -> p e r", e=E),
                                       ALU.mult, ALU.mult).then_inc(wh_ready, 1)
                if ni is not None:
                    add_context(ni, q)
                    take_rest(ni, q, z_hi, z_lo, by_token)
                dve.wait_ge(wh_hi, t1)
                v.tensor_tensor(wh_t[:, 1, :], bank[3][:, 0:P], wh_t[:, 0, :].bitcast(F32),
                                ALU.subtract).then_inc(wh_lo, 1)
                dve.wait_ge(resid_ready, t1)
                for h in range(2):
                    dve.wait_ge(ffn1_done, 4 * i + 2 * p + h + 1)
                    o = resid[:, p, h * HALF:(h + 1) * HALF]
                    v.tensor_tensor(o, bank[4 + 2 * p + h][:, :], o, ALU.add).then_inc(out_ready, 1)

            with dve.Fori(0, PAIRS - 1) as i:
                period1(i, 0, i, 1)
                period1(i, 1, i + 1, 0)
            period1(last, 0, last, 1)
            period1(last, 1, None, None)

        @block.gpsimd
        def _(pool):
            g = nc.gpsimd
            g.memset(agg, 0.0).then_inc(agg_zeroed, 1)

            def add_bias0(i, p, first_tiles=False):
                pool.wait_ge(x_loaded[p], 16 * (i + 1))
                if not first_tiles:
                    pool.wait_ge(x1_stored[p], 16 * i)
                g.tensor_tensor(resid[:, p, :], xs[:, p, :], bias_bc[:, :], ALU.add).then_inc(xb_ready, 2)

            def make_x1(i, p):
                pool.wait_ge(xb_ready, 4 * i + 2 * p + 2)
                for h in range(2):
                    pool.wait_ge(scaled, 4 * i + 2 * p + h + 1)
                    cols = slice(h * HALF, (h + 1) * HALF)
                    g.tensor_tensor(resid[:, p, cols], os_sb[:, cols], resid[:, p, cols], ALU.add).then_inc(x1_ready, 1)

            def rest_of_stage(p, n, rounded, dst, hi):
                pool.wait_ge(stage_hi[p], rounded)
                g.tensor_tensor(dst, stage[:, p, 0:n], hi.bitcast(F32), ALU.subtract).then_inc(stage_lo[p], 1)

            pool.wait_ge(agg_done, 4)
            pool.wait_ge(bias0_loaded, 16)
            add_bias0(0, 0, True)
            add_bias0(0, 1, True)
            rest_of_stage(1, H, 5, band[:, 1, :, :].rearrange("p a n -> p (a n)"),
                          band[:, 0, :, :].rearrange("p a n -> p (a n)"))
            with pool.Fori(0, PAIRS - 1) as i:
                make_x1(i, 0)
                chunk = [early[:, a, bass.ds(i, 1), :].rearrange("p a n -> p (a n)") for a in range(2)]
                rest_of_stage(0, NW, i + 5, chunk[1], chunk[0])
                add_bias0(i + 1, 0)
                make_x1(i, 1)
                add_bias0(i + 1, 1)
            last = PAIRS - 1

            def rest_of_taps(i, p):
                pool.wait_ge(taps_hi, 2 * i + p + 1)
                g.tensor_tensor(taps[:, 1, :, :], raw[:, p, :, :], taps[:, 0, :, :].bitcast(F32),
                                ALU.subtract).then_inc(taps_lo, 2)

            make_x1(last, 0)
            rest_of_taps(0, 0)
            rest_of_stage(0, NW, 12, early[:, 1, L8 - 1, :], early[:, 0, L8 - 1, :])
            rest_of_stage(1, H, 6, lora[:, 1, :], lora[:, 0, :])
            make_x1(last, 1)
            rest_of_taps(0, 1)
            for c in range(L8):
                p = c % 2
                rest_of_stage(p, HALF, (12, 6)[p] + c // 2 + 1, wlate_s[:, 1, c, :], wlate_s[:, 0, c, :])
            pool.wait_ge(bias1_loaded, 16)

            def add_bias1(i, p):
                pool.wait_ge(resid_loaded[p], 16 * (i + 1))
                g.tensor_tensor(resid[:, p, :], resid[:, p, :], bias_bc[:, :], ALU.add).then_inc(resid_ready, 1)

            with pool.Fori(0, PAIRS - 1) as i:
                for p in range(2):
                    add_bias1(i, p)
                    rest_of_taps(i + 1, p)
            add_bias1(last, 0)
            add_bias1(last, 1)


_INS = ["x", "consts", "rows", "mix", "wsign", "scales", "bias0", "toep", "wearly", "wlate", "bm", "bias1"]


def lay_out(a):
    import numpy as np
    f = {k: np.asarray(v) for k, v in a.items()}
    z = lambda *s: np.zeros(s, np.float32)
    perm = lambda w, axis: np.moveaxis(np.moveaxis(w, axis, -1).reshape(*np.moveaxis(w, axis, -1).shape[:-1], P, L8)
                                       .swapaxes(-1, -2).reshape(np.moveaxis(w, axis, -1).shape), -1, axis)
    turned = lambda w: w.reshape(w.shape[0], P, L8).transpose(1, 2, 0)
    consts = z(P, C_END)
    consts[:, C_W0:C_W0 + P] = f["L0_cond_W0"]
    consts[:, C_W1:C_W1 + P] = f["L0_cond_W1"]
    consts[:, C_W2:C_W2 + K8] = f["L0_cond_W2"]
    consts[:, C_CW:C_CW + S] = f["L1_cond_c_weight"].T
    consts[:, C_CT:C_CT + B] = f["cond_128"].T
    consts[:, C_B0] = f["L0_cond_b0"]
    consts[:, C_B1] = f["L0_cond_b1"]
    consts[:, C_GATE:C_GATE + L8 * E] = turned(f["L0_ffn_gate_w"]).reshape(P, L8 * E)
    consts[:, C_ID:C_ID + P] = np.eye(P, dtype=np.float32)
    rows = z(64, R_END)
    rows[0:B, R_B2:R_B2 + K8] = f["L0_cond_b2"]
    rows[0:B, R_FS:R_FS + S] = f["fside_S_0"]
    rows[0:K8, R_BK:R_BK + S] = f["L0_cond_bias_k"]
    is_lo = (np.arange(64) // E) % 2
    rows[:, R_LO] = is_lo
    rows[:, R_SG] = 1 - 2 * is_lo
    mix = f["L0_cond_weight"].reshape(K8, S * S)
    scales = np.concatenate([np.tile(perm(f["L0_ffn_in_channel_scale"], 1), (4, 1)),
                             np.tile(perm(f["L0_ffn_out_channel_scale"], 1), (4, 1))])
    wsign = turned(perm(f["L0_ffn_weight"], 0))
    cw = f["L1_cond_weight"].reshape(GROUPS, CG, CG, TAPS)
    toep = z(2, L8, CG, GROUPS, L8, CG)
    for l in range(L8):
        for k in range(TAPS):
            m = l + k
            toep[m // L8, m % L8, :, :, l, :] = cw[:, :, :, k].transpose(2, 0, 1)
    toep = toep.transpose(1, 2, 0, 3, 4, 5).reshape(P, 2 * GROUPS * P)
    w1 = turned(perm(f["L1_ffn_W"], 0))
    wearly = np.concatenate([turned(f["L1_ffn_Wq"]), turned(f["L1_ffn_Wk"]),
                             turned(f["L1_ffn_A"].reshape(NA, H)), w1[:, :, 0:HALF]], axis=2)
    bm = perm(f["L1_ffn_Bm"], 1).transpose(0, 2, 1).reshape(NA, H)
    return dict(x=perm(f["x"], 2).reshape(TILES * P, H), consts=consts, rows=rows, mix=mix, wsign=wsign,
                scales=scales, bias0=perm(f["L0_ffn_bias"], 0)[None], toep=toep, wearly=wearly,
                wlate=w1[:, :, HALF:], bm=bm, bias1=perm(f["L1_ffn_b"], 0)[None])


def kernel(**inputs):
    import numpy as np
    import concourse.bacc as bacc
    from concourse.bass_utils import run_bass_kernel_spmd

    nc = bacc.Bacc("TRN2", target_bir_lowering=False, num_devices=1)
    given = lay_out(inputs)
    arrays, args = {}, []
    for name in _INS:
        a = np.ascontiguousarray(given[name])
        arrays[f"in_{name}"] = a
        args.append(nc.dram_tensor(f"in_{name}", a.shape, mybir.dt.from_np(a.dtype), kind="ExternalInput").ap())
    out = nc.dram_tensor("out_tokens", (TILES * P, H), F32, kind="ExternalOutput").ap()
    adaln_ffn_kernel(nc, *args, out)
    r = run_bass_kernel_spmd(nc, [arrays], core_ids=[0])
    got = r.results[0]["out_tokens"]
    return got.reshape(B, S, L8, P).swapaxes(2, 3).reshape(B, S, H)
```

```python
from contextlib import ExitStack

import concourse.bass as bass
from concourse import mybir

F32 = mybir.dt.float32
F32R = mybir.dt.float32r
ALU = mybir.AluOpType
ACT = mybir.ActivationFunctionType
AX = mybir.AxisListType

P = 128
B, S, H = 32, 64, 1024
TILES = B * S // P
PAIRS = TILES // 2
L8 = H // P
HALF = 512
E = 8
K8 = 8
R = 16
DK = 32
GROUPS, CG, TAPS = 4, 16, 9
NBG = 2 * GROUPS
NB = P + 1
NQK = 2 * E * DK
NA = E * R
NH = (NQK + NA) // 2
NW = 2 * NH + HALF
C_W0, C_W1, C_W2 = 0, 128, 256
C_CW, C_CT, C_B0, C_B1 = 264, 328, 360, 361
C_GATE, C_ID = 362, 426
C_END = 554
PRODUCTS = ((0, 0), (0, 1), (1, 0))
LOGITS_AT, TURN_AT, SCALES_AT, CONV0_AT = 12, 20, 24, 8
LORA_AT = 11
MIX_AT = (0, 5 * S, 17 * S, 33 * S, 49 * S, 64 * S, 65 * S)
R_B2, R_FS, R_BK, R_LO, R_SG = 0, 8, 72, 136, 137
R_END = 138


def adaln_ffn_kernel(nc, x, consts, rows, mix, wsign, scales, bias0, toep, wearly, wlate, bm, bias1, out):
    x1_dram = nc.dram_tensor("x1_scratch", (TILES * P, H), F32, kind="Internal").ap()
    rows_dram = nc.dram_tensor("token_rows_scratch", (2, B, S), F32, kind="Internal").ap()
    aggb_row = rows_dram[0:1].rearrange("a b s -> a (b s)")
    ctx_row = rows_dram[1:2].rearrange("a b s -> a (b s)")

    ctx = ExitStack()
    with ctx:
        def sb(name, shape, dt=F32):
            return ctx.enter_context(nc.sbuf_tensor(name, shape, dt))

        def sem(name):
            return ctx.enter_context(nc.semaphore(name))

        def sems(name):
            return [sem(f"{name}{p}") for p in range(2)]

        cst = sb("cst", [P, C_END])
        rws = sb("rws", [64, R_END])
        late = sb("late", [P, 2 * L8 * HALF], F32R)
        early = sb("early", [P, 2, L8, NW], F32R)
        lora = sb("lora", [P, 2, H], F32R)
        band = sb("band", [P, 2 * GROUPS, P])
        late_raw = sb("late_raw", [P, 2, H])
        stage = sb("stage", [P, 2, NW])
        scale_w = sb("scale_w", [64, H], F32R)
        parts = sb("parts", [P, 2, 2, L8, P], F32R)
        work = sb("work", [P, 4, H])
        xs = sb("xs", [P, 2, H])
        shared = sb("shared", [P, 2 * NBG * NB])
        bias_bc = sb("bias_bc", [P, H])
        row_bc = sb("row_bc", [P, 2, P])
        routing = sb("routing", [P, 4, 4, E], F32R)
        routing_t = sb("routing_t", [64, P], F32R)
        gate = sb("gate", [P, 64])
        qk = sb("qk", [P, 2, NQK // 2])
        wh = sb("wh", [P, NA])
        wh_t = sb("wh_t", [P, 2, P], F32R)
        hid = sb("hid", [P, 2, B])
        att = sb("att", [B, 64])
        att_t = sb("att_t", [K8, B])
        att_st = sb("att_st", [4 * K8, B], F32R)
        att_parts = sb("att_parts", [B, 2, 2, K8], F32R)
        tok_rows = sb("tok_rows", [B, 2, S])

        signs = late[:, :].rearrange("p (c n) -> p c n", c=L8)
        wlate_s = late[:, :].rearrange("p (a c n) -> p a c n", a=2, c=L8)
        y_t = work[:, 0, :].rearrange("p (c t) -> p c t", c=L8)
        os_sb = work[:, 1, :]
        resid = work[:, 2:4, :]
        mix_raw = work[0:4 * K8, :, :].rearrange("k a n -> k (a n)")
        mix_st = early[0:4 * K8, 0, :, :].rearrange("k a n -> k (a n)")
        agg = shared[:, 0:B * S]
        agg_bo = agg.rearrange("p (b o) -> p b o", b=B)
        raw = shared[:, :].rearrange("p (a n r) -> p a n r", a=2, n=NBG)
        late_src = [late_raw[:, 0, :], late_raw[:, 1, :], stage[:, 1, 0:H], xs[:, 0, :]]
        ident = cst[:, C_ID:C_ID + P]

        bank = [ctx.enter_context(nc.psum_tensor(f"bank{k}", [P, HALF], F32)) for k in range(8)]

        consts_loaded = sem("consts_loaded")
        rows_loaded = sem("rows_loaded")
        mix_loaded = sem("mix_loaded")
        scales_loaded = sem("scales_loaded")
        bias0_loaded = sem("bias0_loaded")
        bias1_loaded = sem("bias1_loaded")
        x_loaded = sems("x_loaded")
        aggb_loaded = sems("aggb_loaded")
        ctx_loaded = sems("ctx_loaded")
        stage_loaded = sems("stage_loaded")
        stage_hi = sems("stage_hi")
        stage_lo = sems("stage_lo")
        rows_stored = sem("rows_stored")

        mlp_done = sem("mlp_done")
        mlp_act = sem("mlp_act")
        ctx_done = sem("ctx_done")
        att_step = sem("att_step")
        att_exp = sem("att_exp")
        att_turned = sem("att_turned")
        att_t_ready = sem("att_t_ready")
        aggb_done = sem("aggb_done")
        tok_rows_ready = sem("tok_rows_ready")
        att_hi = sem("att_hi")
        att_split = sem("att_split")
        att_st_turned = sem("att_st_turned")
        att_st_ready = sem("att_st_ready")
        mix_hi = sem("mix_hi")
        mix_ready = sem("mix_ready")
        agg_zeroed = sem("agg_zeroed")
        agg_done = sem("agg_done")
        agg_ready = sem("agg_ready")
        scale_hi = sem("scale_hi")
        scale_ready = sem("scale_ready")

        y_done = sem("y_done")
        y_biased = sem("y_biased")
        logits_done = sem("logits_done")
        gate_max = sem("gate_max")
        gate_exp = sem("gate_exp")
        gate_rcp = sem("gate_rcp")
        gate_prob = sem("gate_prob")
        routing_zeroed = sem("routing_zeroed")
        routing_hi = sem("routing_hi")
        routing_ready = sem("routing_ready")
        routing_turned = sem("routing_turned")
        routing_copied = sem("routing_copied")
        in_scale_done = sem("in_scale_done")
        out_scale_done = sem("out_scale_done")
        u_ready = sem("u_ready")
        u_hi = sem("u_hi")
        u_lo = sem("u_lo")
        ffn0_done = sem("ffn0_done")
        out_scale_ready = sem("out_scale_ready")
        scaled = sem("scaled")
        xb_ready = sem("xb_ready")
        x1_ready = sem("x1_ready")
        x1_stored = sems("x1_stored")

        pads_zeroed = sem("pads_zeroed")
        raw_loaded = sems("raw_loaded")
        conv_done = sem("conv_done")
        z_biased = sem("z_biased")
        z_hi = sem("z_hi")
        z_lo = sem("z_lo")
        qk_done = sem("qk_done")
        k_copied = sem("k_copied")
        qk_mult = sem("qk_mult")
        scores_ready = sem("scores_ready")
        score_max = sem("score_max")
        score_exp = sem("score_exp")
        score_rcp = sem("score_rcp")
        weights_ready = sem("weights_ready")
        wh_ready = sem("wh_ready")
        wh_turned = sem("wh_turned")
        wh_hi = sem("wh_hi")
        wh_lo = sem("wh_lo")
        ffn1_done = sem("ffn1_done")
        band_loaded = sem("band_loaded")
        late_loaded = [sem(f"late_loaded{k}") for k in range(4)]
        late_hi = sem("late_hi")
        late_lo = sem("late_lo")
        resid_loaded = sems("resid_loaded")
        resid_ready = sem("resid_ready")
        out_ready = sem("out_ready")
        out_stored = sems("out_stored")

        block = ctx.enter_context(nc.Block())

        def tile_rows(dram, t):
            return dram[bass.ds(t * P, P), :]

        @block.sync
        def _(sp):
            def load_x(i, p):
                sp.dma_start(xs[:, p, :], tile_rows(x, 2 * i + p)).then_inc(x_loaded[p], 16)

            def load_row(row, i, p, loaded):
                src = row[0:1, bass.ds((2 * i + p) * P, P)]
                sp.dma_start(row_bc[:, p, :], src.broadcast_to([P, P])).then_inc(loaded[p], 16)

            def load_stage(p, src, n):
                sp.dma_start(stage[:, p, 0:n], src).then_inc(stage_loaded[p], 16)

            sp.dma_start(cst[:, :], consts).then_inc(consts_loaded, 16)
            sp.dma_start(rws[:, :], rows).then_inc(rows_loaded, 16)
            sp.dma_start(bias_bc[0:64, :], scales).then_inc(scales_loaded, 16)
            load_x(0, 0)
            load_x(0, 1)
            for c in range(2):
                load_stage(c, wsign[:, c, :], H)
            sp.wait_ge(scale_ready, 1)
            sp.dma_start(bias_bc[:, :], bias0.broadcast_to([P, H])).then_inc(bias0_loaded, 16)
            sp.wait_ge(tok_rows_ready, 2)
            sp.dma_start(rows_dram.rearrange("a b s -> b a s"), tok_rows[:, :, :]).then_inc(rows_stored, 16)
            sp.wait_ge(rows_stored, 16)
            load_row(aggb_row, 0, 0, aggb_loaded)
            load_row(aggb_row, 0, 1, aggb_loaded)
            sp.wait_ge(stage_hi[0], 4)
            load_stage(0, wearly[:, 0, :], NW)
            sp.wait_ge(stage_hi[1], 4)
            load_stage(1, bm, H)
            sp.dma_start(band[:, :, :].rearrange("p a n -> p (a n)"), toep).then_inc(band_loaded, 16)
            late_pairs = wlate.rearrange("q (k c) n -> k q (c n)", c=2)
            for k in range(2):
                sp.dma_start(late_raw[:, k, :], late_pairs[k]).then_inc(late_loaded[k], 16)

            def store_x1(i, p, both):
                sp.wait_ge(x1_ready, both)
                sp.dma_start(tile_rows(x1_dram, 2 * i + p), resid[:, p, :]).then_inc(x1_stored[p], 16)

            def load_next(i, p, both):
                sp.wait_ge(xb_ready, both)
                sp.wait_ge(y_biased, both)
                load_x(i + 1, p)
                load_row(aggb_row, i + 1, p, aggb_loaded)

            sp.wait_ge(stage_hi[1], 5)
            sp.wait_ge(stage_lo[1], 1)
            sp.dma_start(stage[:, 1, 0:H], late_pairs[2]).then_inc(late_loaded[2], 16)
            with sp.Fori(0, PAIRS - 1) as i:
                load_next(i, 0, 4 * i + 2)
                store_x1(i, 0, 4 * i + 2)
                load_next(i, 1, 4 * i + 4)
                sp.wait_ge(stage_hi[0], i + 5)
                sp.wait_ge(stage_lo[0], i + 1)
                load_stage(0, wearly[:, bass.ds(i + 1, 1), :].rearrange("p a n -> p (a n)"), NW)
                store_x1(i, 1, 4 * i + 4)

            last = PAIRS - 1
            for p in range(2):
                sp.wait_ge(y_biased, 4 * last + 2 * p + 2)
                load_row(ctx_row, 0, p, ctx_loaded)

            def load_raw(i, p):
                sp.wait_ge(x1_stored[p], 16 * (i + 1))
                src = tile_rows(x1_dram, 2 * i + p).rearrange("(n c) (l q) -> l c n q", c=CG, l=L8)
                half = L8 // 2
                for lo in range(2):
                    for l in range(half):
                        part = (lo * half + l) * CG
                        at = 1 - lo
                        sp.dma_start(raw[part:part + CG, p, :, at:at + P],
                                     src[(1 - lo) * half + l]).then_inc(raw_loaded[p], 16)

            sp.wait_ge(pads_zeroed, 2)
            load_raw(0, 0)
            load_raw(0, 1)
            sp.wait_ge(xb_ready, 2 * TILES)
            sp.dma_start(bias_bc[:, :], bias1.broadcast_to([P, H])).then_inc(bias1_loaded, 16)
            sp.dma_start(xs[:, 0, :], late_pairs[3]).then_inc(late_loaded[3], 16)
            store_x1(last, 0, 4 * last + 2)
            store_x1(last, 1, 4 * last + 4)

            def load_resid(i, p):
                sp.dma_start(resid[:, p, :], tile_rows(x1_dram, 2 * i + p)).then_inc(resid_loaded[p], 16)

            for p in range(2):
                sp.wait_ge(x1_stored[p], 16 * PAIRS)
                load_resid(0, p)

            def store_out(i, p, both):
                sp.wait_ge(out_ready, both)
                sp.dma_start(tile_rows(out, 2 * i + p), resid[:, p, :]).then_inc(out_stored[p], 16)

            with sp.Fori(0, PAIRS - 1) as i:
                for p in range(2):
                    both = 4 * i + 2 * p + 2
                    sp.wait_ge(z_biased, both)
                    load_raw(i + 1, p)
                    load_row(ctx_row, i + 1, p, ctx_loaded)
                    store_out(i, p, both)
                    sp.wait_ge(out_stored[p], 16 * (i + 1))
                    load_resid(i + 1, p)
            store_out(last, 0, 4 * last + 2)
            for h in range(2):
                sp.wait_ge(out_ready, 4 * last + 3 + h)
                cols = slice(h * HALF, (h + 1) * HALF)
                sp.dma_start(tile_rows(out, TILES - 1)[:, cols], resid[:, 1, cols]).then_inc(out_stored[1], 16)
            for p in range(2):
                sp.wait_ge(out_stored[p], 16 * (PAIRS + p))

        @block.tensor
        def _(pe):
            mm = nc.tensor.matmul
            pe.wait_ge(consts_loaded, 16)
            mm(bank[0][:, 0:B], cst[:, C_W0:C_W0 + P], cst[:, C_CT:C_CT + B], start=True, stop=True).then_inc(mlp_done, 1)
            mm(bank[1][0:B, 0:S], cst[:, C_CT:C_CT + B], cst[:, C_CW:C_CW + S], start=True, stop=True).then_inc(ctx_done, 1)
            pe.wait_ge(mlp_act, 1)
            mm(bank[0][:, B:2 * B], cst[:, C_W1:C_W1 + P], hid[:, 0, :], start=True, stop=True).then_inc(mlp_done, 1)
            pe.wait_ge(mlp_act, 2)
            mm(bank[2][0:B, 0:K8], hid[:, 1, :], cst[:, C_W2:C_W2 + K8], start=True, stop=True).then_inc(mlp_done, 1)
            pe.wait_ge(att_split, 1)
            nc.tensor.transpose(bank[2][0:4 * K8, 0:B], att_parts[:, :, :, :].bitcast(F32).rearrange("b i j k -> b (i j k)"),
                                ident[0:B, 0:B]).then_inc(att_st_turned, 1)
            nc.tensor.transpose(bank[3][0:K8, 0:B], att[:, 32:32 + K8], ident[0:B, 0:B]).then_inc(att_turned, 1)
            pe.wait_ge(att_st_ready, 1)
            for o in range(S):
                k, at = 4 + o // 16, (o % 16) * B
                pe.wait_ge(mix_ready, next(n for n, end in enumerate(MIX_AT) if end >= (o + 2) * S))
                last = mm(bank[k][:, at:at + B], mix_st[:, o * S:(o + 2) * S], att_st[:, :], start=True, stop=True)
                if o % 16 == 15:
                    last.then_inc(agg_done, 1)
                if o == 15:
                    pe.wait_ge(att_t_ready, 1)
                    mm(bank[0][0:B, 0:S], att_t[:, :], rws[0:K8, R_BK:R_BK + S], start=True, stop=True).then_inc(aggb_done, 1)

            def product_y(i, p, b0=0):
                pe.wait_ge(x_loaded[p], 16 * (i + 1))
                for h in range(2):
                    for c in range(4):
                        at = (4 * h + c) * P
                        last = mm(bank[b0 + h][:, c * P:(c + 1) * P], xs[:, p, at:at + P],
                                  agg[:, bass.ds((2 * i + p) * P, P)], start=True, stop=True)
                    last.then_inc(y_done, 1)

            def product_logits(i, p):
                for c in range(L8):
                    if c % 4 == 0:
                        pe.wait_ge(y_biased, 4 * i + 2 * p + 1 + c // 4)
                    last = mm(bank[2][:, 0:E], y_t[:, c, :], cst[:, C_GATE + c * E:C_GATE + (c + 1) * E],
                              start=(c == 0), stop=(c == L8 - 1))
                last.then_inc(logits_done, 1)

            def turn_routing(i, p):
                pe.wait_ge(routing_ready, 2 * i + p + 1)
                nc.tensor.transpose(bank[3][:, 0:P], routing[:, :, :, :].bitcast(F32).rearrange("p a b e -> p (a b e)"),
                                    ident).then_inc(routing_turned, 1)

            def product_in_scale(i, p):
                pe.wait_ge(routing_copied, 2 * i + p + 1)
                for h in range(2):
                    for c in range(4):
                        at = (4 * h + c) * P
                        last = mm(bank[2 + h][:, c * P:(c + 1) * P], scale_w[0:32, at:at + P], routing_t[0:32, :],
                                  start=True, stop=True)
                    last.then_inc(in_scale_done, 1)

            def product_out_scale():
                for h in range(2):
                    mm(bank[6 + h][:, :], routing_t[32:64, :], scale_w[32:64, h * HALF:(h + 1) * HALF],
                       start=True, stop=True).then_inc(out_scale_done, 1)

            def ffn0_step(i, p, k, first_tile=False):
                h, c, a = k // 16, k % 16 // 8 * 4 + k % 4, k % 8 // 4
                if k in (0, 8):
                    pe.wait_ge(u_hi, 4 * i + 2 * p + 1 + k // 8)
                if k in (4, 12):
                    pe.wait_ge(u_lo, 4 * i + 2 * p + 1 + k // 8)
                if k % 16 == 0 and not first_tile:
                    pe.wait_ge(scaled, 4 * i + 2 * p - 1 + h)
                if first_tile and h == 0 and a == 0:
                    pe.wait_ge(stage_hi[c % 2], c // 2 + 1)
                last = mm(bank[4 + h][:, :], parts[:, p, a, c, :], signs[:, c, h * HALF:(h + 1) * HALF],
                          start=(k % 16 == 0), stop=(k % 16 == 15))
                if k % 16 == 15:
                    last.then_inc(ffn0_done, 1)

            pe.wait_ge(agg_ready, 8)
            product_y(0, 0)
            product_y(0, 1, 6)
            product_logits(0, 0)
            pe.wait_ge(scale_ready, 1)
            pe.wait_ge(routing_zeroed, 1)
            turn_routing(0, 0)
            product_in_scale(0, 0)

            def period0(i, p, ni, q, first_tile=False):
                if not first_tile:
                    pe.wait_ge(y_biased, 4 * i + 2 * p + 2)
                    product_y(ni, q)
                for k in range(32):
                    if k == LOGITS_AT:
                        pe.wait_ge(u_ready, 4 * i + 2 * p + 2)
                        product_logits(ni, q)
                    if k == TURN_AT:
                        turn_routing(ni, q)
                    if k == SCALES_AT:
                        pe.wait_ge(out_scale_ready, 4 * i + 2 * p + 2)
                        product_in_scale(ni, q)
                        product_out_scale()
                    if k == LOGITS_AT // 2 and first_tile:
                        pe.wait_ge(y_biased, 4)
                        product_out_scale()
                    ffn0_step(i, p, k, first_tile)

            period0(0, 0, 0, 1, True)
            period0(0, 1, 1, 0)
            with pe.Fori(1, PAIRS - 1) as i:
                period0(i, 0, i, 1)
                period0(i, 1, i + 1, 0)
            last_i = PAIRS - 1
            period0(last_i, 0, last_i, 1)

            def product_conv(i, p):
                pe.wait_ge(raw_loaded[p], (i + 1) * (16 * L8))
                for n in range(NBG):
                    for s in range(2):
                        last = mm(bank[n // 4][:, (n % 4) * P:(n % 4 + 1) * P], raw[:, p, n, s:s + P],
                                  band[:, s * GROUPS + n % 4, :], start=(s == 0), stop=(s == 1))
                    if n % 4 == 3:
                        last.then_inc(conv_done, 1)

            for k in range(32):
                if k == CONV0_AT:
                    pe.wait_ge(y_biased, 2 * TILES)
                    pe.wait_ge(band_loaded, 16)
                    pe.wait_ge(pads_zeroed, 2)
                    product_conv(0, 0)
                ffn0_step(last_i, 1, k)

            def z_step(dst, w, p, k, close=True):
                c, (a, b) = k // 3, PRODUCTS[k % 3]
                return mm(dst, parts[:, p, a, c, :], w(b, c), start=(k == 0), stop=(close and k == 23))

            def period1(i, p, ni, q, late_ready=None):
                pe.wait_ge(z_hi, 4 * i + 2 * p + 2)
                pe.wait_ge(z_lo, 4 * i + 2 * p + 2)
                for h in range(2):
                    for k in range(24):
                        last = z_step(bank[2 + h][:, 0:NH], lambda b, c: early[:, b, c, h * NH:(h + 1) * NH], p, k)
                    last.then_inc(qk_done, 1)
                if ni is not None:
                    product_conv(ni, q)
                if late_ready:
                    pe.wait_ge(scaled, 2 * TILES)
                    pe.wait_ge(out_scale_ready, 2 * TILES)
                o = [bank[4 + 2 * p], bank[5 + 2 * p]]
                for k in range(24):
                    z_step(o[0][:, :], lambda b, c: early[:, b, c, 2 * NH:NW], p, k, False)
                pe.wait_ge(wh_ready, 2 * i + p + 1)
                nc.tensor.transpose(bank[3][:, NH:NH + P], wh[:, :], ident).then_inc(wh_turned, 1)
                if late_ready:
                    pe.wait_ge(late_hi, 4)
                    pe.wait_ge(late_lo, 4)
                def add_lora(h):
                    for k, (a, b) in enumerate(PRODUCTS):
                        last = mm(o[h][:, :], wh_t[:, a, :], lora[:, b, h * HALF:(h + 1) * HALF],
                                  start=False, stop=(k == 2))
                    last.then_inc(ffn1_done, 1)

                for k in range(24):
                    z_step(o[1][:, :], lambda b, c: wlate_s[:, b, c, :], p, k, False)
                    if k == LORA_AT:
                        pe.wait_ge(wh_hi, 2 * i + p + 1)
                        pe.wait_ge(wh_lo, 2 * i + p + 1)
                        add_lora(0)
                add_lora(1)

            pe.wait_ge(stage_hi[0], 12)
            pe.wait_ge(stage_lo[0], 8)
            pe.wait_ge(stage_hi[1], 5)
            pe.wait_ge(stage_lo[1], 1)
            pe.wait_ge(z_biased, 2)
            pe.wait_ge(u_ready, 2 * TILES)
            period1(0, 0, 0, 1, True)

            def gates(i, p):
                pe.wait_ge(qk_mult, 2 * i + p)
                pe.wait_ge(z_biased, 4 * i + 2 * p + 2)

            gates(0, 1)
            period1(0, 1, 1, 0)
            with pe.Fori(1, PAIRS - 1) as i:
                for p in range(2):
                    gates(i, p)
                    pe.wait_ge(out_ready, 4 * i + 2 * p - 2)
                    period1(i, p, i + p, 1 - p)
            gates(last_i, 0)
            pe.wait_ge(out_ready, 4 * last_i - 2)
            period1(last_i, 0, last_i, 1)
            gates(last_i, 1)
            pe.wait_ge(out_ready, 4 * last_i)
            period1(last_i, 1, None, None)

        @block.scalar
        def _(act):
            do = nc.scalar.activation
            act.dma_start(mix_raw, mix).then_inc(mix_loaded, 16)

            def round_mix(k):
                n = MIX_AT[k + 1] - MIX_AT[k]
                src = MIX_AT[k] % (S * S)
                do(mix_st[:, MIX_AT[k]:MIX_AT[k] + n], mix_raw[:, src:src + n], ACT.Copy,
                   scale=rws[0:4 * K8, R_SG:R_SG + 1]).then_inc(mix_hi, 1)

            for k in range(2):
                act.wait_ge(mlp_done, k + 1)
                do(hid[:, k, :], bank[0][:, k * B:(k + 1) * B], ACT.Gelu,
                   bias=cst[:, C_B0 + k:C_B0 + k + 1]).then_inc(mlp_act, 1)
                if k == 0:
                    act.wait_ge(rows_loaded, 16)
                    act.wait_ge(mix_loaded, 16)
                    round_mix(0)
            act.wait_ge(att_step, 2)
            do(att[:, 16:16 + K8], att[:, 0:K8], ACT.Exp, bias=att[:, 8:9], accum_out=att[:, 9:10]).then_inc(att_exp, 1)
            for k in range(1, len(MIX_AT) - 1):
                round_mix(k)
            act.wait_ge(scales_loaded, 16)
            do(scale_w[:, :], bias_bc[0:64, :], ACT.Copy, scale=rws[:, R_SG:R_SG + 1]).then_inc(scale_hi, 1)

            def sign_chunk(c):
                p = c % 2
                act.wait_ge(stage_loaded[p], 16 * (c // 2 + 1))
                do(signs[:, c, :], stage[:, p, 0:H], ACT.Sign).then_inc(stage_hi[p], 1)
                if c + 2 < L8:
                    act.wait_ge(stage_hi[p], c // 2 + 1)
                    act.dma_start(stage[:, p, 0:H], wsign[:, c + 2, :]).then_inc(stage_loaded[p], 16)

            for c in range(L8):
                sign_chunk(c)

            def gate_exps(i, p):
                act.wait_ge(gate_max, 2 * i + p + 1)
                do(gate[:, 8:16], bank[2][:, 0:E], ACT.Exp, bias=gate[:, 0:1], accum_out=gate[:, 1:2]).then_inc(gate_exp, 1)

            def copy_routing(i, p):
                act.wait_ge(routing_turned, 2 * i + p + 1)
                do(routing_t[:, :], bank[3][0:64, 0:P], ACT.Copy).then_inc(routing_copied, 1)

            def round_parts(i, p, ready, done, cols, halves=(0, 1)):
                for h in halves:
                    act.wait_ge(ready, 4 * i + 2 * p + h + 1)
                    do(cols(parts[:, p, 0], h), cols(y_t, h), ACT.Copy).then_inc(done, 1)

            by_block = lambda a, h: a[:, 4 * h:4 * h + 4, :]
            by_token = lambda a, h: a[:, :, 64 * h:64 * h + 64]

            def copy_out_scale(i, p, reused):
                for h in range(2):
                    act.wait_ge(out_scale_done, 4 * i + 2 * p + h + 1)
                    if reused:
                        act.wait_ge(x1_ready, 4 * i + 2 * p - 1 + h)
                    do(os_sb[:, h * HALF:(h + 1) * HALF], bank[6 + h][:, :], ACT.Copy).then_inc(out_scale_ready, 1)

            def round_stage(p, n, loaded, dst):
                act.wait_ge(stage_loaded[p], loaded)
                do(dst, stage[:, p, 0:n], ACT.Copy).then_inc(stage_hi[p], 1)

            def tile0(i, p, reused=True, fresh=False):
                gate_exps(i, p)
                copy_routing(i, p)
                if not fresh:
                    act.wait_ge(ffn0_done, 4 * i + 2 * p - 2)
                round_parts(i, p, u_ready, u_hi, by_block)
                copy_out_scale(i, p, reused)

            tile0(0, 0, False, True)
            round_stage(1, H, 16 * 5, lora[:, 0, :])
            tile0(0, 1, True, True)
            with act.Fori(0, PAIRS - 1) as i:
                round_stage(0, NW, (i + 5) * 16, early[:, 0, bass.ds(i, 1), :].rearrange("p a n -> p (a n)"))
                tile0(i + 1, 0)
                tile0(i + 1, 1)
            round_stage(0, NW, 16 * 12, early[:, 0, L8 - 1, :])
            act.wait_ge(ffn0_done, 2 * TILES - 2)
            round_parts(0, 0, z_biased, z_hi, by_token)
            act.wait_ge(ffn0_done, 2 * TILES)
            for k in range(4):
                act.wait_ge(late_loaded[k], 16)
                do(wlate_s[:, 0, 2 * k:2 * k + 2, :].rearrange("p c n -> p (c n)"), late_src[k],
                   ACT.Copy).then_inc(late_hi, 1)

            def period1(i, p, ni, q):
                nq, n0 = NQK // 2, NH - NQK // 2
                act.wait_ge(qk_done, 4 * i + 2 * p + 1)
                do(qk[:, 0, 0:n0], bank[2][:, nq:NH], ACT.Copy).then_inc(k_copied, 1)
                act.wait_ge(qk_done, 4 * i + 2 * p + 2)
                do(qk[:, 0, n0:nq], bank[3][:, 0:nq - n0], ACT.Copy).then_inc(k_copied, 1)
                act.wait_ge(score_max, 4 * i + 2 * p + 2)
                do(gate[:, 16:24], gate[:, 24:32], ACT.Exp, bias=gate[:, 2:3], scale=float(DK) ** -0.5,
                   accum_out=gate[:, 3:4]).then_inc(score_exp, 1)
                if ni is not None:
                    round_parts(ni, q, z_biased, z_hi, by_token, (0,))
                act.wait_ge(wh_turned, 2 * i + p + 1)
                do(wh_t[:, 0, :], bank[3][:, NH:NH + P], ACT.Copy).then_inc(wh_hi, 1)
                if ni is not None:
                    round_parts(ni, q, z_biased, z_hi, by_token, (1,))

            with act.Fori(0, PAIRS - 1) as i:
                period1(i, 0, i, 1)
                period1(i, 1, i + 1, 0)
            last = PAIRS - 1
            period1(last, 0, last, 1)
            period1(last, 1, None, None)

        @block.vector
        def _(dve):
            v = nc.vector
            dve.wait_ge(rows_loaded, 16)
            dve.wait_ge(ctx_done, 1)
            v.tensor_tensor(tok_rows[:, 1, :], bank[1][0:B, 0:S], rws[0:B, R_FS:R_FS + S], ALU.add).then_inc(tok_rows_ready, 1)
            def rest_of_mix(k):
                dve.wait_ge(mix_hi, k + 1)
                n = MIX_AT[k + 1] - MIX_AT[k]
                dst, src = MIX_AT[k], MIX_AT[k] % (S * S)
                v.scalar_tensor_tensor(mix_st[:, dst:dst + n], mix_raw[:, src:src + n], rws[0:4 * K8, R_LO:R_LO + 1],
                                       mix_st[:, dst:dst + n].bitcast(F32), ALU.mult, ALU.add).then_inc(mix_ready, 1)

            rest_of_mix(0)
            dve.wait_ge(mlp_done, 3)
            v.tensor_tensor(att[:, 0:K8], bank[2][0:B, 0:K8], rws[0:B, R_B2:R_B2 + K8], ALU.add).then_inc(att_step, 1)
            dve.wait_ge(att_step, 1)
            v.tensor_reduce(att[:, 8:9], att[:, 0:K8], AX.X, ALU.max, negate=True).then_inc(att_step, 1)
            dve.wait_ge(att_exp, 1)
            v.reciprocal(att[:, 10:11], att[:, 9:10]).then_inc(att_step, 1)
            dve.wait_ge(att_step, 3)
            v.tensor_scalar(att[:, 32:32 + K8], att[:, 16:16 + K8], att[:, 10:11], None, ALU.mult).then_inc(att_step, 1)
            dve.wait_ge(att_step, 4)
            prob = att[:, 32:32 + K8].rearrange("p (a b e) -> p a b e", a=1, b=1).broadcast_to([B, 1, 2, K8])
            v.tensor_copy(att_parts[:, 0:1, :, :], prob).then_inc(att_hi, 1)
            dve.wait_ge(att_hi, 1)
            v.tensor_tensor(att_parts[:, 1:2, :, :], prob, att_parts[:, 0:1, :, :].bitcast(F32), ALU.subtract).then_inc(att_split, 1)

            dve.wait_ge(att_st_turned, 1)
            v.tensor_copy(att_st[:, :], bank[2][0:4 * K8, 0:B]).then_inc(att_st_ready, 1)
            rest_of_mix(1)
            dve.wait_ge(att_turned, 1)
            v.tensor_copy(att_t[:, :], bank[3][0:K8, 0:B]).then_inc(att_t_ready, 1)
            rest_of_mix(2)
            dve.wait_ge(aggb_done, 1)
            v.tensor_copy(tok_rows[:, 0, :], bank[0][0:B, 0:S]).then_inc(tok_rows_ready, 1)
            for k in range(3, len(MIX_AT) - 1):
                rest_of_mix(k)
            dve.wait_ge(scale_hi, 1)
            v.scalar_tensor_tensor(scale_w[:, :], bias_bc[0:64, :], rws[:, R_LO:R_LO + 1], scale_w[:, :].bitcast(F32),
                                   ALU.mult, ALU.add).then_inc(scale_ready, 1)
            v.memset(routing[:, 2:4, :, :].bitcast(F32), 0.0).then_inc(routing_zeroed, 1)
            dve.wait_ge(agg_zeroed, 1)
            for k in range(4):
                dve.wait_ge(agg_done, k + 1)
                src = bank[4 + k][0:64, :].rearrange("p (o b) -> p b o", b=B)
                v.tensor_copy(agg_bo[0:64, 0::2, 16 * k:16 * k + 16], src[:, 0::2, :]).then_inc(agg_ready, 1)
                src = bank[4 + k][64:128, :].rearrange("p (o b) -> p b o", b=B)
                n = 16 if k < 3 else 15
                ins = v.tensor_copy(agg_bo[64:128, 1::2, 16 * k + 1:16 * k + 1 + n], src[:, 1::2, 0:n])
                if k == 3:
                    ins = v.tensor_copy(agg_bo[64:128, 1::2, 0:1], src[:, 1::2, 15:16])
                ins.then_inc(agg_ready, 1)


            def add_mix_bias(i, p, first_tile=False, b0=0):
                dve.wait_ge(aggb_loaded[p], 16 * (i + 1))
                if not first_tile:
                    dve.wait_ge(u_lo, 4 * i + 2 * p)
                for h in range(2):
                    dve.wait_ge(y_done, 4 * i + 2 * p + h + 1)
                    v.tensor_tensor(y_t[:, 4 * h:4 * h + 4, :], bank[b0 + h][:, :].rearrange("p (c t) -> p c t", c=4),
                                    row_bc[:, p:p + 1, :].broadcast_to([P, 4, P]), ALU.add).then_inc(y_biased, 1)

            def route(i, p):
                t1 = 2 * i + p + 1
                dve.wait_ge(logits_done, t1)
                v.tensor_reduce(gate[:, 0:1], bank[2][:, 0:E], AX.X, ALU.max, negate=True).then_inc(gate_max, 1)
                dve.wait_ge(gate_exp, t1)
                v.reciprocal(gate[:, 4:5], gate[:, 1:2]).then_inc(gate_rcp, 1)
                dve.wait_ge(gate_rcp, t1)
                dve.wait_ge(routing_ready, t1 - 1)
                v.tensor_scalar(gate[:, 32:40], gate[:, 8:16], gate[:, 4:5], None, ALU.mult).then_inc(gate_prob, 1)
                dve.wait_ge(gate_prob, t1)
                prob = gate[:, 32:40].rearrange("p (a b e) -> p a b e", a=1, b=1).broadcast_to([P, 2, 2, E])
                v.tensor_copy(routing[:, 0:2, 0:2, :], prob).then_inc(routing_hi, 1)
                dve.wait_ge(routing_hi, t1)
                v.tensor_tensor(routing[:, 0:2, 2:4, :], prob, routing[:, 0:2, 0:2, :].bitcast(F32),
                                ALU.subtract).then_inc(routing_ready, 1)

            def scale_in(i, p):
                for h in range(2):
                    dve.wait_ge(in_scale_done, 4 * i + 2 * p + h + 1)
                    y_h = y_t[:, 4 * h:4 * h + 4, :]
                    v.tensor_tensor(y_h, bank[2 + h][:, :].rearrange("p (c t) -> p c t", c=4), y_h,
                                    ALU.mult).then_inc(u_ready, 1)

            def take_rest(i, p, rounded, done, cols, halves=(0, 1)):
                for h in halves:
                    dve.wait_ge(rounded, 4 * i + 2 * p + h + 1)
                    v.tensor_tensor(cols(parts[:, p, 1], h), cols(y_t, h), cols(parts[:, p, 0], h).bitcast(F32),
                                    ALU.subtract).then_inc(done, 1)

            def scale_out(i, p, h):
                dve.wait_ge(ffn0_done, 4 * i + 2 * p + h + 1)
                dve.wait_ge(out_scale_ready, 4 * i + 2 * p + h + 1)
                o = os_sb[:, h * HALF:(h + 1) * HALF]
                v.tensor_tensor(o, bank[4 + h][:, :], o, ALU.mult).then_inc(scaled, 1)

            by_block = lambda a, h: a[:, 4 * h:4 * h + 4, :]
            by_token = lambda a, h: a[:, :, 64 * h:64 * h + 64]

            def period0(i, p, ni, q, last_y=False, b0=0):
                add_mix_bias(ni, q, b0=b0)
                if last_y:
                    v.memset(raw[0:64, :, :, 0:1], 0.0).then_inc(pads_zeroed, 1)
                    v.memset(raw[64:128, :, :, P:NB], 0.0).then_inc(pads_zeroed, 1)
                route(ni, q)
                scale_out(i, p, 0)
                scale_in(ni, q)
                take_rest(ni, q, u_hi, u_lo, by_block)
                scale_out(i, p, 1)

            add_mix_bias(0, 0, True)
            route(0, 0)
            scale_in(0, 0)
            take_rest(0, 0, u_hi, u_lo, by_block)
            period0(0, 0, 0, 1, b0=6)
            period0(0, 1, 1, 0)
            with dve.Fori(1, PAIRS - 1) as i:
                period0(i, 0, i, 1)
                period0(i, 1, i + 1, 0)
            last = PAIRS - 1
            period0(last, 0, last, 1, True)

            def add_context(i, p, halves=(0, 1)):
                dve.wait_ge(ctx_loaded[p], 16 * (i + 1))
                dve.wait_ge(z_lo, 4 * i + 2 * p)
                for h in halves:
                    dve.wait_ge(conv_done, 4 * i + 2 * p + h + 1)
                    zt = y_t[:, :, 64 * h:64 * h + 64].rearrange("p l (n c) -> p n l c", c=CG)
                    add = row_bc[:, p:p + 1, 64 * h:64 * h + 64].rearrange("p l (n c) -> p n l c", c=CG)
                    v.tensor_tensor(zt, bank[h][:, :].rearrange("p (n l c) -> p n l c", n=4, l=L8),
                                    add.broadcast_to([P, 4, L8, CG]), ALU.add).then_inc(z_biased, 1)

            dve.wait_ge(u_lo, 2 * TILES)
            add_context(0, 0)
            take_rest(0, 0, z_hi, z_lo, by_token)
            scale_out(last, 1, 0)
            scale_out(last, 1, 1)

            def rest_of_late(k):
                dve.wait_ge(late_hi, k + 1)
                cols = slice(2 * k, 2 * k + 2)
                hi, lo = (wlate_s[:, a, cols, :].rearrange("p c n -> p (c n)") for a in range(2))
                v.tensor_tensor(lo, late_src[k], hi.bitcast(F32), ALU.subtract).then_inc(late_lo, 1)

            rest_of_late(1)
            rest_of_late(3)

            def period1(i, p, ni, q):
                t1 = 2 * i + p + 1
                dve.wait_ge(k_copied, 2 * t1)
                v.tensor_tensor(qk[:, 1, :], bank[2][:, 0:NQK // 2], qk[:, 0, :], ALU.mult).then_inc(qk_mult, 1)
                dve.wait_ge(qk_mult, t1)
                v.tensor_reduce(gate[:, 24:32], qk[:, 1, :].rearrange("p (e d) -> p e d", e=E), AX.X,
                                ALU.add).then_inc(scores_ready, 1)
                dve.wait_ge(scores_ready, t1)
                v.tensor_reduce(gate[:, 5:6], gate[:, 24:32], AX.X, ALU.max, negate=True).then_inc(score_max, 1)
                dve.wait_ge(score_max, 2 * t1 - 1)
                v.tensor_scalar(gate[:, 2:3], gate[:, 5:6], float(DK) ** -0.5, None, ALU.mult).then_inc(score_max, 1)
                dve.wait_ge(score_exp, t1)
                v.reciprocal(gate[:, 6:7], gate[:, 3:4]).then_inc(score_rcp, 1)
                dve.wait_ge(score_rcp, t1)
                w = gate[:, 16:24].rearrange("p (e a) -> p e a", a=1).broadcast_to([P, E, R])
                v.scalar_tensor_tensor(wh[:, :].rearrange("p (e r) -> p e r", e=E), w, gate[:, 6:7],
                                       bank[3][:, NH - NA:NH].rearrange("p (e r) -> p e r", e=E),
                                       ALU.mult, ALU.mult).then_inc(wh_ready, 1)
                if ni is not None:
                    add_context(ni, q, (0,))
                dve.wait_ge(wh_hi, t1)
                v.tensor_tensor(wh_t[:, 1, :], bank[3][:, NH:NH + P], wh_t[:, 0, :].bitcast(F32),
                                ALU.subtract).then_inc(wh_lo, 1)
                if ni is not None:
                    take_rest(ni, q, z_hi, z_lo, by_token, (0,))
                    add_context(ni, q, (1,))
                    take_rest(ni, q, z_hi, z_lo, by_token, (1,))
                dve.wait_ge(resid_ready, t1)
                for h in range(2):
                    dve.wait_ge(ffn1_done, 4 * i + 2 * p + h + 1)
                    o = resid[:, p, h * HALF:(h + 1) * HALF]
                    v.tensor_tensor(o, bank[4 + 2 * p + h][:, :], o, ALU.add).then_inc(out_ready, 1)

            with dve.Fori(0, PAIRS - 1) as i:
                period1(i, 0, i, 1)
                period1(i, 1, i + 1, 0)
            period1(last, 0, last, 1)
            period1(last, 1, None, None)

        @block.gpsimd
        def _(pool):
            g = nc.gpsimd
            g.memset(agg, 0.0).then_inc(agg_zeroed, 1)

            def add_bias0(i, p, first_tiles=False):
                pool.wait_ge(x_loaded[p], 16 * (i + 1))
                if not first_tiles:
                    pool.wait_ge(x1_stored[p], 16 * i)
                g.tensor_tensor(resid[:, p, :], xs[:, p, :], bias_bc[:, :], ALU.add).then_inc(xb_ready, 2)

            def make_x1(i, p):
                pool.wait_ge(xb_ready, 4 * i + 2 * p + 2)
                for h in range(2):
                    pool.wait_ge(scaled, 4 * i + 2 * p + h + 1)
                    cols = slice(h * HALF, (h + 1) * HALF)
                    g.tensor_tensor(resid[:, p, cols], os_sb[:, cols], resid[:, p, cols], ALU.add).then_inc(x1_ready, 1)

            def rest_of_stage(p, n, rounded, dst, hi):
                pool.wait_ge(stage_hi[p], rounded)
                g.tensor_tensor(dst, stage[:, p, 0:n], hi.bitcast(F32), ALU.subtract).then_inc(stage_lo[p], 1)

            pool.wait_ge(agg_done, 4)
            pool.wait_ge(bias0_loaded, 16)
            add_bias0(0, 0, True)
            add_bias0(0, 1, True)
            rest_of_stage(1, H, 5, lora[:, 1, :], lora[:, 0, :])
            with pool.Fori(0, PAIRS - 1) as i:
                make_x1(i, 0)
                chunk = [early[:, a, bass.ds(i, 1), :].rearrange("p a n -> p (a n)") for a in range(2)]
                rest_of_stage(0, NW, i + 5, chunk[1], chunk[0])
                add_bias0(i + 1, 0)
                make_x1(i, 1)
                add_bias0(i + 1, 1)
            last = PAIRS - 1

            make_x1(last, 0)
            rest_of_stage(0, NW, 12, early[:, 1, L8 - 1, :], early[:, 0, L8 - 1, :])
            make_x1(last, 1)
            for k in (0, 2):
                pool.wait_ge(late_hi, k + 1)
                hi, lo = (wlate_s[:, a, 2 * k:2 * k + 2, :].rearrange("p c n -> p (c n)") for a in range(2))
                g.tensor_tensor(lo, late_src[k], hi.bitcast(F32), ALU.subtract).then_inc(late_lo, 1)
            pool.wait_ge(bias1_loaded, 16)

            def add_bias1(i, p):
                pool.wait_ge(resid_loaded[p], 16 * (i + 1))
                g.tensor_tensor(resid[:, p, :], resid[:, p, :], bias_bc[:, :], ALU.add).then_inc(resid_ready, 1)

            with pool.Fori(0, PAIRS - 1) as i:
                for p in range(2):
                    add_bias1(i, p)
            add_bias1(last, 0)
            add_bias1(last, 1)


_INS = ["x", "consts", "rows", "mix", "wsign", "scales", "bias0", "toep", "wearly", "wlate", "bm", "bias1"]


def lay_out(a):
    import numpy as np
    f = {k: np.asarray(v) for k, v in a.items()}
    z = lambda *s: np.zeros(s, np.float32)
    perm = lambda w, axis: np.moveaxis(np.moveaxis(w, axis, -1).reshape(*np.moveaxis(w, axis, -1).shape[:-1], P, L8)
                                       .swapaxes(-1, -2).reshape(np.moveaxis(w, axis, -1).shape), -1, axis)
    turned = lambda w: w.reshape(w.shape[0], P, L8).transpose(1, 2, 0)
    consts = z(P, C_END)
    consts[:, C_W0:C_W0 + P] = f["L0_cond_W0"]
    consts[:, C_W1:C_W1 + P] = f["L0_cond_W1"]
    consts[:, C_W2:C_W2 + K8] = f["L0_cond_W2"]
    consts[:, C_CW:C_CW + S] = f["L1_cond_c_weight"].T
    consts[:, C_CT:C_CT + B] = f["cond_128"].T
    consts[:, C_B0] = f["L0_cond_b0"]
    consts[:, C_B1] = f["L0_cond_b1"]
    consts[:, C_GATE:C_GATE + L8 * E] = turned(f["L0_ffn_gate_w"]).reshape(P, L8 * E)
    consts[:, C_ID:C_ID + P] = np.eye(P, dtype=np.float32)
    rows = z(64, R_END)
    rows[0:B, R_B2:R_B2 + K8] = f["L0_cond_b2"]
    rows[0:B, R_FS:R_FS + S] = f["fside_S_0"]
    rows[0:K8, R_BK:R_BK + S] = f["L0_cond_bias_k"]
    is_lo = (np.arange(64) // E) % 2
    rows[:, R_LO] = is_lo
    rows[:, R_SG] = 1 - 2 * is_lo
    mix = np.tile(f["L0_cond_weight"].reshape(K8, S * S), (4, 1))
    scales = np.concatenate([np.tile(perm(f["L0_ffn_in_channel_scale"], 1), (4, 1)),
                             np.tile(perm(f["L0_ffn_out_channel_scale"], 1), (4, 1))])
    wsign = turned(perm(f["L0_ffn_weight"], 0))
    cw = f["L1_cond_weight"].reshape(GROUPS, CG, CG, TAPS)
    toep = z(2, L8, CG, GROUPS, L8, CG)
    for l in range(L8):
        for k in range(TAPS):
            m = l + k
            toep[m // L8, m % L8, :, :, l, :] = cw[:, :, :, k].transpose(2, 0, 1)
    toep = toep.transpose(1, 2, 0, 3, 4, 5).reshape(P, 2 * GROUPS * P)
    w1 = turned(perm(f["L1_ffn_W"], 0))
    wearly = np.concatenate([turned(f["L1_ffn_Wq"]), turned(f["L1_ffn_Wk"]),
                             turned(f["L1_ffn_A"].reshape(NA, H)), w1[:, :, 0:HALF]], axis=2)
    bm = perm(f["L1_ffn_Bm"], 1).transpose(0, 2, 1).reshape(NA, H)
    return dict(x=perm(f["x"], 2).reshape(TILES * P, H), consts=consts, rows=rows, mix=mix, wsign=wsign,
                scales=scales, bias0=perm(f["L0_ffn_bias"], 0)[None], toep=toep, wearly=wearly,
                wlate=w1[:, :, HALF:], bm=bm, bias1=perm(f["L1_ffn_b"], 0)[None])


def kernel(**inputs):
    import numpy as np
    import concourse.bacc as bacc
    from concourse.bass_utils import run_bass_kernel_spmd

    nc = bacc.Bacc("TRN2", target_bir_lowering=False, num_devices=1)
    given = lay_out(inputs)
    arrays, args = {}, []
    for name in _INS:
        a = np.ascontiguousarray(given[name])
        arrays[f"in_{name}"] = a
        args.append(nc.dram_tensor(f"in_{name}", a.shape, mybir.dt.from_np(a.dtype), kind="ExternalInput").ap())
    out = nc.dram_tensor("out_tokens", (TILES * P, H), F32, kind="ExternalOutput").ap()
    adaln_ffn_kernel(nc, *args, out)
    r = run_bass_kernel_spmd(nc, [arrays], core_ids=[0])
    got = r.results[0]["out_tokens"]
    return got.reshape(B, S, L8, P).swapaxes(2, 3).reshape(B, S, H)
```

```python
from contextlib import ExitStack

import concourse.bass as bass
from concourse import mybir

F32 = mybir.dt.float32
F32R = mybir.dt.float32r
ALU = mybir.AluOpType
ACT = mybir.ActivationFunctionType
AX = mybir.AxisListType

P = 128
B, S, H = 32, 64, 1024
TILES = B * S // P
PAIRS = TILES // 2
L8 = H // P
HALF = 512
E = 8
K8 = 8
R = 16
DK = 32
GROUPS, CG, TAPS = 4, 16, 9
NBG = 2 * GROUPS
NB = P + 1
NQK = 2 * E * DK
NA = E * R
NH = (NQK + NA) // 2
NW = 2 * NH + HALF
C_W0, C_W1, C_W2 = 0, 128, 256
C_CW, C_CT, C_B0, C_B1 = 264, 328, 360, 361
C_GATE, C_ID = 362, 426
C_END = 554
PRODUCTS = ((0, 0), (0, 1), (1, 0))
LOGITS_AT, TURN_AT, SCALES_AT, CONV0_AT = 12, 20, 24, 8
SIGNS_FIRST = 6
LORA_AT = 11
R_B2, R_FS, R_BK, R_LO, R_SG = 0, 8, 72, 136, 137
R_HALF, R_TILE, R_END = 138, 266, 394


def adaln_ffn_kernel(nc, x, consts, rows, mix, wsign, scales, bias0, toep, wearly, wlate, bm, bias1, out):
    x1_dram = nc.dram_tensor("x1_scratch", (TILES * P, H), F32, kind="Internal").ap()
    rows_dram = nc.dram_tensor("token_rows_scratch", (2, B, S), F32, kind="Internal").ap()
    aggb_row = rows_dram[0:1].rearrange("a b s -> a (b s)")
    ctx_row = rows_dram[1:2].rearrange("a b s -> a (b s)")

    ctx = ExitStack()
    with ctx:
        def sb(name, shape, dt=F32):
            return ctx.enter_context(nc.sbuf_tensor(name, shape, dt))

        def sem(name):
            return ctx.enter_context(nc.semaphore(name))

        def sems(name):
            return [sem(f"{name}{p}") for p in range(2)]

        cst = sb("cst", [P, C_END])
        rws = sb("rws", [64, R_END])
        late = sb("late", [P, 2 * L8 * HALF], F32R)
        early = sb("early", [P, 2, L8, NW], F32R)
        lora = sb("lora", [P, 2, H], F32R)
        band = sb("band", [P, 2 * GROUPS, P])
        late_raw = sb("late_raw", [P, 2, H])
        stage = sb("stage", [P, 2, NW])
        scale_w = sb("scale_w", [64, H], F32R)
        parts = sb("parts", [P, 2, 2, L8, P], F32R)
        work = sb("work", [P, 4, H])
        xs = sb("xs", [P, 2, H])
        raw = sb("raw", [P, 2, NBG, NB])
        mix_w = sb("mix_w", [P, S, K8])
        weighted = sb("weighted", [P, S, K8])
        agg = sb("agg", [P, 2, P])
        att_bc = sb("att_bc", [P, TILES, K8])
        bias_bc = sb("bias_bc", [P, H])
        row_bc = sb("row_bc", [P, 2, P])
        routing = sb("routing", [P, 4, 4, E], F32R)
        routing_t = sb("routing_t", [64, P], F32R)
        gate = sb("gate", [P, 64])
        qk = sb("qk", [P, 2, NQK // 2])
        wh = sb("wh", [P, NA])
        wh_t = sb("wh_t", [P, 2, P], F32R)
        hid = sb("hid", [P, 2, B])
        att = sb("att", [B, 64])
        att_t = sb("att_t", [K8, B])
        tok_rows = sb("tok_rows", [B, 2, S])

        signs = late[:, :].rearrange("p (c n) -> p c n", c=L8)
        wlate_s = late[:, :].rearrange("p (a c n) -> p a c n", a=2, c=L8)
        y_t = work[:, 0, :].rearrange("p (c t) -> p c t", c=L8)
        os_sb = work[:, 1, :]
        resid = work[:, 2:4, :]
        sign_src = [stage[:, 0, 0:H], stage[:, 1, 0:H], late_raw[:, 0, :], late_raw[:, 1, :], os_sb,
                    band[:, :, :].rearrange("p a n -> p (a n)"), resid[:, 0, :], resid[:, 1, :]]
        att_tiles = wh[0:B, :].rearrange("b (t k) -> b t k", t=TILES)
        att_rep = qk[0:K8, :, :].rearrange("k a n -> k (a n)").rearrange("k (b r) -> k b r", b=4)
        late_src = [late_raw[:, 0, :], late_raw[:, 1, :], stage[:, 1, 0:H], xs[:, 0, :]]
        ident = cst[:, C_ID:C_ID + P]

        bank = [ctx.enter_context(nc.psum_tensor(f"bank{k}", [P, HALF], F32)) for k in range(8)]

        consts_loaded = sem("consts_loaded")
        rows_loaded = sem("rows_loaded")
        mix_loaded = sem("mix_loaded")
        scales_loaded = sem("scales_loaded")
        bias0_loaded = sem("bias0_loaded")
        bias1_loaded = sem("bias1_loaded")
        x_loaded = sems("x_loaded")
        aggb_loaded = sems("aggb_loaded")
        ctx_loaded = sems("ctx_loaded")
        stage_loaded = sems("stage_loaded")
        stage_hi = sems("stage_hi")
        stage_lo = sems("stage_lo")
        rows_stored = sem("rows_stored")

        mlp_done = sem("mlp_done")
        mlp_act = sem("mlp_act")
        ctx_done = sem("ctx_done")
        att_step = sem("att_step")
        att_exp = sem("att_exp")
        att_turned = sem("att_turned")
        att_t_ready = sem("att_t_ready")
        aggb_done = sem("aggb_done")
        tok_rows_ready = sem("tok_rows_ready")
        att_rep_ready = sem("att_rep_ready")
        att_tiled = sem("att_tiled")
        att_spread = sem("att_spread")
        att_bc_ready = sem("att_bc_ready")
        first_rows_done = sem("first_rows_done")
        first_rows_ready = sem("first_rows_ready")
        sign_loaded = [sem(f"sign_loaded{c}") for c in range(L8)]
        signs_ready = sem("signs_ready")
        agg_weighted = sem("agg_weighted")
        agg_zeroed = sem("agg_zeroed")
        agg_ready = sem("agg_ready")
        scale_hi = sem("scale_hi")
        scale_ready = sem("scale_ready")

        y_done = sem("y_done")
        y_biased = sem("y_biased")
        logits_done = sem("logits_done")
        gate_max = sem("gate_max")
        gate_exp = sem("gate_exp")
        gate_rcp = sem("gate_rcp")
        gate_prob = sem("gate_prob")
        routing_zeroed = sem("routing_zeroed")
        routing_hi = sem("routing_hi")
        routing_ready = sem("routing_ready")
        routing_turned = sem("routing_turned")
        routing_copied = sem("routing_copied")
        in_scale_done = sem("in_scale_done")
        out_scale_done = sem("out_scale_done")
        u_ready = sem("u_ready")
        u_hi = sem("u_hi")
        u_lo = sem("u_lo")
        ffn0_done = sem("ffn0_done")
        out_scale_ready = sem("out_scale_ready")
        scaled = sem("scaled")
        xb_ready = sem("xb_ready")
        x1_ready = sem("x1_ready")
        x1_stored = sems("x1_stored")

        pads_zeroed = sem("pads_zeroed")
        raw_loaded = sems("raw_loaded")
        conv_done = sem("conv_done")
        z_biased = sem("z_biased")
        z_hi = sem("z_hi")
        z_lo = sem("z_lo")
        qk_done = sem("qk_done")
        k_copied = sem("k_copied")
        qk_mult = sem("qk_mult")
        scores_ready = sem("scores_ready")
        score_max = sem("score_max")
        score_exp = sem("score_exp")
        score_rcp = sem("score_rcp")
        weights_ready = sem("weights_ready")
        wh_ready = sem("wh_ready")
        wh_turned = sem("wh_turned")
        wh_hi = sem("wh_hi")
        wh_lo = sem("wh_lo")
        ffn1_done = sem("ffn1_done")
        band_loaded = sem("band_loaded")
        late_loaded = [sem(f"late_loaded{k}") for k in range(4)]
        late_hi = sem("late_hi")
        late_lo = sem("late_lo")
        resid_loaded = sems("resid_loaded")
        resid_ready = sem("resid_ready")
        out_ready = sem("out_ready")
        out_stored = sems("out_stored")

        block = ctx.enter_context(nc.Block())

        def tile_rows(dram, t):
            return dram[bass.ds(t * P, P), :]

        @block.sync
        def _(sp):
            def load_x(i, p):
                sp.dma_start(xs[:, p, :], tile_rows(x, 2 * i + p)).then_inc(x_loaded[p], 16)

            def load_row(row, i, p, loaded):
                src = row[0:1, bass.ds((2 * i + p) * P, P)]
                sp.dma_start(row_bc[:, p, :], src.broadcast_to([P, P])).then_inc(loaded[p], 16)

            def load_stage(p, src, n):
                sp.dma_start(stage[:, p, 0:n], src).then_inc(stage_loaded[p], 16)

            sp.dma_start(cst[:, :], consts).then_inc(consts_loaded, 16)
            sp.dma_start(rws[:, :], rows).then_inc(rows_loaded, 16)
            load_x(0, 0)
            sp.dma_start(bias_bc[0:64, :], scales).then_inc(scales_loaded, 16)
            load_x(0, 1)
            for c in range(L8):
                sp.dma_start(sign_src[c], wsign[:, c, :]).then_inc(sign_loaded[c], 16)
            sp.wait_ge(scale_ready, 1)
            sp.dma_start(bias_bc[:, :], bias0.broadcast_to([P, H])).then_inc(bias0_loaded, 16)
            sp.wait_ge(tok_rows_ready, 2)
            sp.dma_start(rows_dram.rearrange("a b s -> b a s"), tok_rows[:, :, :]).then_inc(rows_stored, 16)
            late_pairs = wlate.rearrange("q (k c) n -> k q (c n)", c=2)
            sp.wait_ge(signs_ready, 1)
            load_stage(0, wearly[:, 0, :], NW)
            sp.wait_ge(signs_ready, 2)
            load_stage(1, bm, H)
            for k in range(2):
                sp.wait_ge(signs_ready, 3 + k)
                sp.dma_start(late_raw[:, k, :], late_pairs[k]).then_inc(late_loaded[k], 16)
            sp.wait_ge(signs_ready, 6)
            sp.dma_start(band[:, :, :].rearrange("p a n -> p (a n)"), toep).then_inc(band_loaded, 16)
            sp.wait_ge(rows_stored, 16)

            def store_x1(i, p, both):
                sp.wait_ge(x1_ready, both)
                sp.dma_start(tile_rows(x1_dram, 2 * i + p), resid[:, p, :]).then_inc(x1_stored[p], 16)

            def load_next(i, p, both):
                sp.wait_ge(xb_ready, both)
                sp.wait_ge(y_biased, both)
                load_x(i + 1, p)
                load_row(aggb_row, i + 1, p, aggb_loaded)

            with sp.Fori(0, PAIRS - 1) as i:
                load_next(i, 0, 4 * i + 2)
                store_x1(i, 0, 4 * i + 2)
                load_next(i, 1, 4 * i + 4)
                sp.wait_ge(stage_hi[0], i + 1)
                sp.wait_ge(stage_lo[0], i + 1)
                load_stage(0, wearly[:, bass.ds(i + 1, 1), :].rearrange("p a n -> p (a n)"), NW)
                store_x1(i, 1, 4 * i + 4)

            sp.wait_ge(stage_hi[1], 1)
            sp.wait_ge(stage_lo[1], 1)
            sp.dma_start(stage[:, 1, 0:H], late_pairs[2]).then_inc(late_loaded[2], 16)

            last = PAIRS - 1
            for p in range(2):
                sp.wait_ge(y_biased, 4 * last + 2 * p + 2)
                load_row(ctx_row, 0, p, ctx_loaded)

            def load_raw(i, p):
                sp.wait_ge(x1_stored[p], 16 * (i + 1))
                src = tile_rows(x1_dram, 2 * i + p).rearrange("(n c) (l q) -> l c n q", c=CG, l=L8)
                half = L8 // 2
                for lo in range(2):
                    for l in range(half):
                        part = (lo * half + l) * CG
                        at = 1 - lo
                        sp.dma_start(raw[part:part + CG, p, :, at:at + P],
                                     src[(1 - lo) * half + l]).then_inc(raw_loaded[p], 16)

            sp.wait_ge(pads_zeroed, 2)
            load_raw(0, 0)
            load_raw(0, 1)
            sp.wait_ge(xb_ready, 2 * TILES)
            sp.dma_start(bias_bc[:, :], bias1.broadcast_to([P, H])).then_inc(bias1_loaded, 16)
            sp.dma_start(xs[:, 0, :], late_pairs[3]).then_inc(late_loaded[3], 16)
            store_x1(last, 0, 4 * last + 2)
            store_x1(last, 1, 4 * last + 4)

            def load_resid(i, p):
                sp.dma_start(resid[:, p, :], tile_rows(x1_dram, 2 * i + p)).then_inc(resid_loaded[p], 16)

            for p in range(2):
                sp.wait_ge(x1_stored[p], 16 * PAIRS)
                load_resid(0, p)

            def store_out(i, p, both):
                sp.wait_ge(out_ready, both)
                sp.dma_start(tile_rows(out, 2 * i + p), resid[:, p, :]).then_inc(out_stored[p], 16)

            with sp.Fori(0, PAIRS - 1) as i:
                for p in range(2):
                    both = 4 * i + 2 * p + 2
                    sp.wait_ge(z_biased, both)
                    load_raw(i + 1, p)
                    load_row(ctx_row, i + 1, p, ctx_loaded)
                    store_out(i, p, both)
                    sp.wait_ge(out_stored[p], 16 * (i + 1))
                    load_resid(i + 1, p)
            store_out(last, 0, 4 * last + 2)
            for h in range(2):
                sp.wait_ge(out_ready, 4 * last + 3 + h)
                cols = slice(h * HALF, (h + 1) * HALF)
                sp.dma_start(tile_rows(out, TILES - 1)[:, cols], resid[:, 1, cols]).then_inc(out_stored[1], 16)
            for p in range(2):
                sp.wait_ge(out_stored[p], 16 * (PAIRS + p))

        @block.tensor
        def _(pe):
            mm = nc.tensor.matmul
            pe.wait_ge(consts_loaded, 16)
            mm(bank[0][:, 0:B], cst[:, C_W0:C_W0 + P], cst[:, C_CT:C_CT + B], start=True, stop=True).then_inc(mlp_done, 1)
            mm(bank[1][0:B, 0:S], cst[:, C_CT:C_CT + B], cst[:, C_CW:C_CW + S], start=True, stop=True).then_inc(ctx_done, 1)
            pe.wait_ge(mlp_act, 1)
            mm(bank[0][:, B:2 * B], cst[:, C_W1:C_W1 + P], hid[:, 0, :], start=True, stop=True).then_inc(mlp_done, 1)
            pe.wait_ge(mlp_act, 2)
            mm(bank[2][0:B, 0:K8], hid[:, 1, :], cst[:, C_W2:C_W2 + K8], start=True, stop=True).then_inc(mlp_done, 1)
            pe.wait_ge(att_tiled, 1)
            mm(bank[2][:, 0:P], rws[0:B, R_HALF:R_HALF + P], wh[0:B, :], start=True, stop=True).then_inc(att_spread, 1)
            nc.tensor.transpose(bank[3][0:K8, 0:B], att[:, 32:32 + K8], ident[0:B, 0:B]).then_inc(att_turned, 1)
            bias_k = rws[0:K8, R_BK:R_BK + S]
            pe.wait_ge(att_rep_ready, 1)
            for b in range(4):
                last = mm(bank[4][:, b * S:(b + 1) * S], att_rep[:, b, :], bias_k, start=True, stop=True)
            last.then_inc(first_rows_done, 1)
            pe.wait_ge(att_t_ready, 1)
            mm(bank[5][0:B, 0:S], att_t[:, :], bias_k, start=True, stop=True).then_inc(aggb_done, 1)

            def product_y(i, p, b0=0):
                pe.wait_ge(x_loaded[p], 16 * (i + 1))
                pe.wait_ge(agg_ready, 4 * i + 2 * p + 2)
                for h in range(2):
                    for c in range(4):
                        at = (4 * h + c) * P
                        last = mm(bank[b0 + h][:, c * P:(c + 1) * P], xs[:, p, at:at + P],
                                  agg[:, p, :], start=True, stop=True)
                    last.then_inc(y_done, 1)

            def product_logits(i, p):
                for c in range(L8):
                    if c % 4 == 0:
                        pe.wait_ge(y_biased, 4 * i + 2 * p + 1 + c // 4)
                    last = mm(bank[2][:, 0:E], y_t[:, c, :], cst[:, C_GATE + c * E:C_GATE + (c + 1) * E],
                              start=(c == 0), stop=(c == L8 - 1))
                last.then_inc(logits_done, 1)

            def turn_routing(i, p):
                pe.wait_ge(routing_ready, 2 * i + p + 1)
                nc.tensor.transpose(bank[3][:, 0:P], routing[:, :, :, :].bitcast(F32).rearrange("p a b e -> p (a b e)"),
                                    ident).then_inc(routing_turned, 1)

            def product_in_scale(i, p):
                pe.wait_ge(routing_copied, 2 * i + p + 1)
                for h in range(2):
                    for c in range(4):
                        at = (4 * h + c) * P
                        last = mm(bank[2 + h][:, c * P:(c + 1) * P], scale_w[0:32, at:at + P], routing_t[0:32, :],
                                  start=True, stop=True)
                    last.then_inc(in_scale_done, 1)

            def product_out_scale():
                for h in range(2):
                    mm(bank[6 + h][:, :], routing_t[32:64, :], scale_w[32:64, h * HALF:(h + 1) * HALF],
                       start=True, stop=True).then_inc(out_scale_done, 1)

            def ffn0_step(i, p, k, first_tile=False):
                h, c, a = k // 16, k % 16 // 8 * 4 + k % 4, k % 8 // 4
                if k in (0, 8):
                    pe.wait_ge(u_hi, 4 * i + 2 * p + 1 + k // 8)
                if k in (4, 12):
                    pe.wait_ge(u_lo, 4 * i + 2 * p + 1 + k // 8)
                if k % 16 == 0 and not first_tile:
                    pe.wait_ge(scaled, 4 * i + 2 * p - 1 + h)
                if first_tile and h == 0 and a == 0:
                    pe.wait_ge(signs_ready, c + 1)
                last = mm(bank[4 + h][:, :], parts[:, p, a, c, :], signs[:, c, h * HALF:(h + 1) * HALF],
                          start=(k % 16 == 0), stop=(k % 16 == 15))
                if k % 16 == 15:
                    last.then_inc(ffn0_done, 1)

            product_y(0, 0)
            product_y(0, 1, 6)
            product_logits(0, 0)
            pe.wait_ge(scale_ready, 1)
            pe.wait_ge(routing_zeroed, 1)
            turn_routing(0, 0)
            product_in_scale(0, 0)

            def period0(i, p, ni, q, first_tile=False):
                if not first_tile:
                    pe.wait_ge(y_biased, 4 * i + 2 * p + 2)
                    product_y(ni, q)
                for k in range(32):
                    if k == LOGITS_AT:
                        pe.wait_ge(u_ready, 4 * i + 2 * p + 2)
                        product_logits(ni, q)
                    if k == TURN_AT:
                        turn_routing(ni, q)
                    if k == SCALES_AT:
                        pe.wait_ge(out_scale_ready, 4 * i + 2 * p + 2)
                        product_in_scale(ni, q)
                        product_out_scale()
                    if k == LOGITS_AT - 4 and first_tile:
                        pe.wait_ge(y_biased, 4)
                        product_out_scale()
                    ffn0_step(i, p, k, first_tile)

            period0(0, 0, 0, 1, True)
            period0(0, 1, 1, 0)
            with pe.Fori(1, PAIRS - 1) as i:
                period0(i, 0, i, 1)
                period0(i, 1, i + 1, 0)
            last_i = PAIRS - 1
            period0(last_i, 0, last_i, 1)

            def product_conv(i, p):
                pe.wait_ge(raw_loaded[p], (i + 1) * (16 * L8))
                for n in range(NBG):
                    for s in range(2):
                        last = mm(bank[n // 4][:, (n % 4) * P:(n % 4 + 1) * P], raw[:, p, n, s:s + P],
                                  band[:, s * GROUPS + n % 4, :], start=(s == 0), stop=(s == 1))
                    if n % 4 == 3:
                        last.then_inc(conv_done, 1)

            for k in range(32):
                if k == CONV0_AT:
                    pe.wait_ge(y_biased, 2 * TILES)
                    pe.wait_ge(band_loaded, 16)
                    pe.wait_ge(pads_zeroed, 2)
                    product_conv(0, 0)
                ffn0_step(last_i, 1, k)

            def z_step(dst, w, p, k, close=True):
                c, (a, b) = k // 3, PRODUCTS[k % 3]
                return mm(dst, parts[:, p, a, c, :], w(b, c), start=(k == 0), stop=(close and k == 23))

            def period1(i, p, ni, q, late_ready=None):
                pe.wait_ge(z_hi, 4 * i + 2 * p + 2)
                pe.wait_ge(z_lo, 4 * i + 2 * p + 2)
                for h in range(2):
                    for k in range(24):
                        last = z_step(bank[2 + h][:, 0:NH], lambda b, c: early[:, b, c, h * NH:(h + 1) * NH], p, k)
                    last.then_inc(qk_done, 1)
                if ni is not None:
                    product_conv(ni, q)
                if late_ready:
                    pe.wait_ge(scaled, 2 * TILES)
                    pe.wait_ge(out_scale_ready, 2 * TILES)
                o = [bank[4 + 2 * p], bank[5 + 2 * p]]
                for k in range(24):
                    z_step(o[0][:, :], lambda b, c: early[:, b, c, 2 * NH:NW], p, k, False)
                pe.wait_ge(wh_ready, 2 * i + p + 1)
                nc.tensor.transpose(bank[3][:, NH:NH + P], wh[:, :], ident).then_inc(wh_turned, 1)
                if late_ready:
                    pe.wait_ge(late_hi, 4)
                    pe.wait_ge(late_lo, 4)
                def add_lora(h):
                    for k, (a, b) in enumerate(PRODUCTS):
                        last = mm(o[h][:, :], wh_t[:, a, :], lora[:, b, h * HALF:(h + 1) * HALF],
                                  start=False, stop=(k == 2))
                    last.then_inc(ffn1_done, 1)

                for k in range(24):
                    z_step(o[1][:, :], lambda b, c: wlate_s[:, b, c, :], p, k, False)
                    if k == LORA_AT:
                        pe.wait_ge(wh_hi, 2 * i + p + 1)
                        pe.wait_ge(wh_lo, 2 * i + p + 1)
                        add_lora(0)
                add_lora(1)

            pe.wait_ge(stage_hi[0], 8)
            pe.wait_ge(stage_lo[0], 8)
            pe.wait_ge(stage_hi[1], 1)
            pe.wait_ge(stage_lo[1], 1)
            pe.wait_ge(z_biased, 2)
            pe.wait_ge(u_ready, 2 * TILES)
            period1(0, 0, 0, 1, True)

            def gates(i, p):
                pe.wait_ge(qk_mult, 2 * i + p)
                pe.wait_ge(z_biased, 4 * i + 2 * p + 2)

            gates(0, 1)
            period1(0, 1, 1, 0)
            with pe.Fori(1, PAIRS - 1) as i:
                for p in range(2):
                    gates(i, p)
                    pe.wait_ge(out_ready, 4 * i + 2 * p - 2)
                    period1(i, p, i + p, 1 - p)
            gates(last_i, 0)
            pe.wait_ge(out_ready, 4 * last_i - 2)
            period1(last_i, 0, last_i, 1)
            gates(last_i, 1)
            pe.wait_ge(out_ready, 4 * last_i)
            period1(last_i, 1, None, None)

        @block.scalar
        def _(act):
            do = nc.scalar.activation
            act.dma_start(mix_w[:, :, :], mix).then_inc(mix_loaded, 16)

            for k in range(2):
                act.wait_ge(mlp_done, k + 1)
                do(hid[:, k, :], bank[0][:, k * B:(k + 1) * B], ACT.Gelu,
                   bias=cst[:, C_B0 + k:C_B0 + k + 1]).then_inc(mlp_act, 1)
            act.wait_ge(att_step, 2)
            do(att[:, 16:16 + K8], att[:, 0:K8], ACT.Exp, bias=att[:, 8:9], accum_out=att[:, 9:10]).then_inc(att_exp, 1)
            act.wait_ge(att_turned, 1)
            do(att_rep[:, :, :], bank[3][0:K8, 0:4].rearrange("k (b a) -> k b a", a=1).broadcast_to([K8, 4, P]),
               ACT.Copy).then_inc(att_rep_ready, 1)
            do(att_t[:, :], bank[3][0:K8, 0:B], ACT.Copy).then_inc(att_t_ready, 1)
            act.wait_ge(first_rows_done, 1)
            do(row_bc[:, :, :].rearrange("p a n -> p (a n)"), bank[4][:, 0:2 * P], ACT.Copy).then_inc(first_rows_ready, 1)
            act.wait_ge(rows_loaded, 16)
            act.wait_ge(scales_loaded, 16)
            do(scale_w[:, :], bias_bc[0:64, :], ACT.Copy, scale=rws[:, R_SG:R_SG + 1]).then_inc(scale_hi, 1)

            def take_signs(c):
                act.wait_ge(sign_loaded[c], 16)
                do(signs[:, c, :], sign_src[c], ACT.Sign).then_inc(signs_ready, 1)

            for c in range(SIGNS_FIRST):
                take_signs(c)

            def gate_exps(i, p):
                act.wait_ge(gate_max, 2 * i + p + 1)
                do(gate[:, 8:16], bank[2][:, 0:E], ACT.Exp, bias=gate[:, 0:1], accum_out=gate[:, 1:2]).then_inc(gate_exp, 1)

            def copy_routing(i, p):
                act.wait_ge(routing_turned, 2 * i + p + 1)
                do(routing_t[:, :], bank[3][0:64, 0:P], ACT.Copy).then_inc(routing_copied, 1)

            def round_parts(i, p, ready, done, cols, halves=(0, 1)):
                for h in halves:
                    act.wait_ge(ready, 4 * i + 2 * p + h + 1)
                    do(cols(parts[:, p, 0], h), cols(y_t, h), ACT.Copy).then_inc(done, 1)

            by_block = lambda a, h: a[:, 4 * h:4 * h + 4, :]
            by_token = lambda a, h: a[:, :, 64 * h:64 * h + 64]

            def copy_out_scale(i, p, reused):
                for h in range(2):
                    act.wait_ge(out_scale_done, 4 * i + 2 * p + h + 1)
                    if reused:
                        act.wait_ge(x1_ready, 4 * i + 2 * p - 1 + h)
                    do(os_sb[:, h * HALF:(h + 1) * HALF], bank[6 + h][:, :], ACT.Copy).then_inc(out_scale_ready, 1)

            def round_stage(p, n, loaded, dst):
                act.wait_ge(stage_loaded[p], loaded)
                do(dst, stage[:, p, 0:n], ACT.Copy).then_inc(stage_hi[p], 1)

            def tile0(i, p, reused=True, fresh=False):
                gate_exps(i, p)
                if not reused:
                    take_signs(SIGNS_FIRST)
                copy_routing(i, p)
                if not reused:
                    for c in range(SIGNS_FIRST + 1, L8):
                        take_signs(c)
                    act.wait_ge(signs_ready, L8)
                if not fresh:
                    act.wait_ge(ffn0_done, 4 * i + 2 * p - 2)
                round_parts(i, p, u_ready, u_hi, by_block)
                copy_out_scale(i, p, reused)

            tile0(0, 0, False, True)
            round_stage(1, H, 16, lora[:, 0, :])
            tile0(0, 1, True, True)
            with act.Fori(0, PAIRS - 1) as i:
                round_stage(0, NW, (i + 1) * 16, early[:, 0, bass.ds(i, 1), :].rearrange("p a n -> p (a n)"))
                tile0(i + 1, 0)
                tile0(i + 1, 1)
            round_stage(0, NW, 16 * L8, early[:, 0, L8 - 1, :])
            act.wait_ge(ffn0_done, 2 * TILES - 2)
            round_parts(0, 0, z_biased, z_hi, by_token)
            act.wait_ge(ffn0_done, 2 * TILES)
            for k in range(4):
                act.wait_ge(late_loaded[k], 16)
                do(wlate_s[:, 0, 2 * k:2 * k + 2, :].rearrange("p c n -> p (c n)"), late_src[k],
                   ACT.Copy).then_inc(late_hi, 1)

            def period1(i, p, ni, q):
                nq, n0 = NQK // 2, NH - NQK // 2
                act.wait_ge(qk_done, 4 * i + 2 * p + 1)
                do(qk[:, 0, 0:n0], bank[2][:, nq:NH], ACT.Copy).then_inc(k_copied, 1)
                act.wait_ge(qk_done, 4 * i + 2 * p + 2)
                do(qk[:, 0, n0:nq], bank[3][:, 0:nq - n0], ACT.Copy).then_inc(k_copied, 1)
                act.wait_ge(score_max, 4 * i + 2 * p + 2)
                do(gate[:, 16:24], gate[:, 24:32], ACT.Exp, bias=gate[:, 2:3], scale=float(DK) ** -0.5,
                   accum_out=gate[:, 3:4]).then_inc(score_exp, 1)
                if ni is not None:
                    round_parts(ni, q, z_biased, z_hi, by_token, (0,))
                act.wait_ge(wh_turned, 2 * i + p + 1)
                do(wh_t[:, 0, :], bank[3][:, NH:NH + P], ACT.Copy).then_inc(wh_hi, 1)
                if ni is not None:
                    round_parts(ni, q, z_biased, z_hi, by_token, (1,))

            with act.Fori(0, PAIRS - 1) as i:
                period1(i, 0, i, 1)
                period1(i, 1, i + 1, 0)
            last = PAIRS - 1
            period1(last, 0, last, 1)
            period1(last, 1, None, None)

        @block.vector
        def _(dve):
            v = nc.vector
            v.memset(raw[0:64, :, :, 0:1], 0.0).then_inc(pads_zeroed, 1)
            v.memset(raw[64:128, :, :, P:NB], 0.0).then_inc(pads_zeroed, 1)
            v.memset(agg[:, :, :], 0.0).then_inc(agg_zeroed, 1)
            v.memset(routing[:, 2:4, :, :].bitcast(F32), 0.0).then_inc(routing_zeroed, 1)
            dve.wait_ge(rows_loaded, 16)
            dve.wait_ge(ctx_done, 1)
            v.tensor_tensor(tok_rows[:, 1, :], bank[1][0:B, 0:S], rws[0:B, R_FS:R_FS + S], ALU.add).then_inc(tok_rows_ready, 1)
            dve.wait_ge(mlp_done, 3)
            v.tensor_tensor(att[:, 0:K8], bank[2][0:B, 0:K8], rws[0:B, R_B2:R_B2 + K8], ALU.add).then_inc(att_step, 1)
            dve.wait_ge(att_step, 1)
            v.tensor_reduce(att[:, 8:9], att[:, 0:K8], AX.X, ALU.max, negate=True).then_inc(att_step, 1)
            dve.wait_ge(att_exp, 1)
            v.reciprocal(att[:, 10:11], att[:, 9:10]).then_inc(att_step, 1)
            dve.wait_ge(att_step, 3)
            v.tensor_scalar(att[:, 32:32 + K8], att[:, 16:16 + K8], att[:, 10:11], None, ALU.mult).then_inc(att_step, 1)
            dve.wait_ge(att_step, 4)
            v.tensor_tensor(att_tiles, att[:, 32:32 + K8].rearrange("b (t k) -> b t k", t=1).broadcast_to([B, TILES, K8]),
                            rws[0:B, R_TILE:R_TILE + P].rearrange("b (t k) -> b t k", t=TILES), ALU.mult).then_inc(att_tiled, 1)
            dve.wait_ge(att_spread, 1)
            v.tensor_copy(att_bc[:, :, :].rearrange("p t k -> p (t k)"), bank[2][:, 0:P]).then_inc(att_bc_ready, 1)

            def mix_kernels(i, p, first_tile=False):
                t = 2 * i + p
                if not first_tile:
                    dve.wait_ge(agg_ready, 2 * t)
                v.tensor_tensor(weighted[:, :, :], mix_w[:, :, :], att_bc[:, bass.ds(t, 1), :].broadcast_to([P, S, K8]),
                                ALU.mult).then_inc(agg_weighted, 1)
                dve.wait_ge(agg_weighted, t + 1)
                for h in range(2):
                    rows = slice(h * S, (h + 1) * S)
                    v.tensor_reduce(agg[rows, p, rows], weighted[rows, :, :], AX.X, ALU.add).then_inc(agg_ready, 1)

            dve.wait_ge(mix_loaded, 16)
            dve.wait_ge(att_bc_ready, 1)
            dve.wait_ge(agg_zeroed, 1)
            mix_kernels(0, 0, True)
            mix_kernels(0, 1)
            dve.wait_ge(aggb_done, 1)
            v.tensor_copy(tok_rows[:, 0, :], bank[5][0:B, 0:S]).then_inc(tok_rows_ready, 1)
            dve.wait_ge(scale_hi, 1)
            v.scalar_tensor_tensor(scale_w[:, :], bias_bc[0:64, :], rws[:, R_LO:R_LO + 1], scale_w[:, :].bitcast(F32),
                                   ALU.mult, ALU.add).then_inc(scale_ready, 1)

            def add_mix_bias(i, p, first_tile=False, b0=0, first_rows=False):
                if first_rows:
                    dve.wait_ge(first_rows_ready, 1)
                else:
                    dve.wait_ge(aggb_loaded[p], 16 * i)
                if not first_tile:
                    dve.wait_ge(u_lo, 4 * i + 2 * p)
                for h in range(2):
                    dve.wait_ge(y_done, 4 * i + 2 * p + h + 1)
                    v.tensor_tensor(y_t[:, 4 * h:4 * h + 4, :], bank[b0 + h][:, :].rearrange("p (c t) -> p c t", c=4),
                                    row_bc[:, p:p + 1, :].broadcast_to([P, 4, P]), ALU.add).then_inc(y_biased, 1)

            def route(i, p):
                t1 = 2 * i + p + 1
                dve.wait_ge(logits_done, t1)
                v.tensor_reduce(gate[:, 0:1], bank[2][:, 0:E], AX.X, ALU.max, negate=True).then_inc(gate_max, 1)
                dve.wait_ge(gate_exp, t1)
                v.reciprocal(gate[:, 4:5], gate[:, 1:2]).then_inc(gate_rcp, 1)
                dve.wait_ge(gate_rcp, t1)
                dve.wait_ge(routing_ready, t1 - 1)
                v.tensor_scalar(gate[:, 32:40], gate[:, 8:16], gate[:, 4:5], None, ALU.mult).then_inc(gate_prob, 1)
                dve.wait_ge(gate_prob, t1)
                prob = gate[:, 32:40].rearrange("p (a b e) -> p a b e", a=1, b=1).broadcast_to([P, 2, 2, E])
                v.tensor_copy(routing[:, 0:2, 0:2, :], prob).then_inc(routing_hi, 1)
                dve.wait_ge(routing_hi, t1)
                v.tensor_tensor(routing[:, 0:2, 2:4, :], prob, routing[:, 0:2, 0:2, :].bitcast(F32),
                                ALU.subtract).then_inc(routing_ready, 1)

            def scale_in(i, p):
                for h in range(2):
                    dve.wait_ge(in_scale_done, 4 * i + 2 * p + h + 1)
                    y_h = y_t[:, 4 * h:4 * h + 4, :]
                    v.tensor_tensor(y_h, bank[2 + h][:, :].rearrange("p (c t) -> p c t", c=4), y_h,
                                    ALU.mult).then_inc(u_ready, 1)

            def take_rest(i, p, rounded, done, cols, halves=(0, 1)):
                for h in halves:
                    dve.wait_ge(rounded, 4 * i + 2 * p + h + 1)
                    v.tensor_tensor(cols(parts[:, p, 1], h), cols(y_t, h), cols(parts[:, p, 0], h).bitcast(F32),
                                    ALU.subtract).then_inc(done, 1)

            def scale_out(i, p, h):
                dve.wait_ge(ffn0_done, 4 * i + 2 * p + h + 1)
                dve.wait_ge(out_scale_ready, 4 * i + 2 * p + h + 1)
                o = os_sb[:, h * HALF:(h + 1) * HALF]
                v.tensor_tensor(o, bank[4 + h][:, :], o, ALU.mult).then_inc(scaled, 1)

            by_block = lambda a, h: a[:, 4 * h:4 * h + 4, :]
            by_token = lambda a, h: a[:, :, 64 * h:64 * h + 64]

            def period0(i, p, ni, q, mix_next=True, first=False):
                add_mix_bias(ni, q, b0=6 if first else 0, first_rows=first)
                if mix_next:
                    mix_kernels(i + 1, p)
                route(ni, q)
                scale_out(i, p, 0)
                scale_in(ni, q)
                take_rest(ni, q, u_hi, u_lo, by_block)
                scale_out(i, p, 1)

            add_mix_bias(0, 0, True, first_rows=True)
            route(0, 0)
            scale_in(0, 0)
            take_rest(0, 0, u_hi, u_lo, by_block)
            period0(0, 0, 0, 1, first=True)
            period0(0, 1, 1, 0)
            with dve.Fori(1, PAIRS - 1) as i:
                period0(i, 0, i, 1)
                period0(i, 1, i + 1, 0)
            last = PAIRS - 1
            period0(last, 0, last, 1, False)

            def add_context(i, p, halves=(0, 1)):
                dve.wait_ge(ctx_loaded[p], 16 * (i + 1))
                dve.wait_ge(z_lo, 4 * i + 2 * p)
                for h in halves:
                    dve.wait_ge(conv_done, 4 * i + 2 * p + h + 1)
                    zt = y_t[:, :, 64 * h:64 * h + 64].rearrange("p l (n c) -> p n l c", c=CG)
                    add = row_bc[:, p:p + 1, 64 * h:64 * h + 64].rearrange("p l (n c) -> p n l c", c=CG)
                    v.tensor_tensor(zt, bank[h][:, :].rearrange("p (n l c) -> p n l c", n=4, l=L8),
                                    add.broadcast_to([P, 4, L8, CG]), ALU.add).then_inc(z_biased, 1)

            dve.wait_ge(u_lo, 2 * TILES)
            add_context(0, 0)
            take_rest(0, 0, z_hi, z_lo, by_token)
            scale_out(last, 1, 0)
            scale_out(last, 1, 1)

            def rest_of_late(k):
                dve.wait_ge(late_hi, k + 1)
                cols = slice(2 * k, 2 * k + 2)
                hi, lo = (wlate_s[:, a, cols, :].rearrange("p c n -> p (c n)") for a in range(2))
                v.tensor_tensor(lo, late_src[k], hi.bitcast(F32), ALU.subtract).then_inc(late_lo, 1)

            rest_of_late(1)
            rest_of_late(3)

            def period1(i, p, ni, q):
                t1 = 2 * i + p + 1
                dve.wait_ge(k_copied, 2 * t1)
                v.tensor_tensor(qk[:, 1, :], bank[2][:, 0:NQK // 2], qk[:, 0, :], ALU.mult).then_inc(qk_mult, 1)
                dve.wait_ge(qk_mult, t1)
                v.tensor_reduce(gate[:, 24:32], qk[:, 1, :].rearrange("p (e d) -> p e d", e=E), AX.X,
                                ALU.add).then_inc(scores_ready, 1)
                dve.wait_ge(scores_ready, t1)
                v.tensor_reduce(gate[:, 5:6], gate[:, 24:32], AX.X, ALU.max, negate=True).then_inc(score_max, 1)
                dve.wait_ge(score_max, 2 * t1 - 1)
                v.tensor_scalar(gate[:, 2:3], gate[:, 5:6], float(DK) ** -0.5, None, ALU.mult).then_inc(score_max, 1)
                dve.wait_ge(score_exp, t1)
                v.reciprocal(gate[:, 6:7], gate[:, 3:4]).then_inc(score_rcp, 1)
                dve.wait_ge(score_rcp, t1)
                w = gate[:, 16:24].rearrange("p (e a) -> p e a", a=1).broadcast_to([P, E, R])
                v.scalar_tensor_tensor(wh[:, :].rearrange("p (e r) -> p e r", e=E), w, gate[:, 6:7],
                                       bank[3][:, NH - NA:NH].rearrange("p (e r) -> p e r", e=E),
                                       ALU.mult, ALU.mult).then_inc(wh_ready, 1)
                if ni is not None:
                    add_context(ni, q, (0,))
                dve.wait_ge(wh_hi, t1)
                v.tensor_tensor(wh_t[:, 1, :], bank[3][:, NH:NH + P], wh_t[:, 0, :].bitcast(F32),
                                ALU.subtract).then_inc(wh_lo, 1)
                if ni is not None:
                    take_rest(ni, q, z_hi, z_lo, by_token, (0,))
                    add_context(ni, q, (1,))
                    take_rest(ni, q, z_hi, z_lo, by_token, (1,))
                dve.wait_ge(resid_ready, t1)
                for h in range(2):
                    dve.wait_ge(ffn1_done, 4 * i + 2 * p + h + 1)
                    o = resid[:, p, h * HALF:(h + 1) * HALF]
                    v.tensor_tensor(o, bank[4 + 2 * p + h][:, :], o, ALU.add).then_inc(out_ready, 1)

            with dve.Fori(0, PAIRS - 1) as i:
                period1(i, 0, i, 1)
                period1(i, 1, i + 1, 0)
            period1(last, 0, last, 1)
            period1(last, 1, None, None)

        @block.gpsimd
        def _(pool):
            g = nc.gpsimd
            def add_bias0(i, p, first_tiles=False):
                pool.wait_ge(x_loaded[p], 16 * (i + 1))
                if not first_tiles:
                    pool.wait_ge(x1_stored[p], 16 * i)
                g.tensor_tensor(resid[:, p, :], xs[:, p, :], bias_bc[:, :], ALU.add).then_inc(xb_ready, 2)

            def make_x1(i, p):
                pool.wait_ge(xb_ready, 4 * i + 2 * p + 2)
                for h in range(2):
                    pool.wait_ge(scaled, 4 * i + 2 * p + h + 1)
                    cols = slice(h * HALF, (h + 1) * HALF)
                    g.tensor_tensor(resid[:, p, cols], os_sb[:, cols], resid[:, p, cols], ALU.add).then_inc(x1_ready, 1)

            def rest_of_stage(p, n, rounded, dst, hi):
                pool.wait_ge(stage_hi[p], rounded)
                g.tensor_tensor(dst, stage[:, p, 0:n], hi.bitcast(F32), ALU.subtract).then_inc(stage_lo[p], 1)

            pool.wait_ge(signs_ready, L8)
            pool.wait_ge(bias0_loaded, 16)
            add_bias0(0, 0, True)
            add_bias0(0, 1, True)
            rest_of_stage(1, H, 1, lora[:, 1, :], lora[:, 0, :])
            with pool.Fori(0, PAIRS - 1) as i:
                make_x1(i, 0)
                chunk = [early[:, a, bass.ds(i, 1), :].rearrange("p a n -> p (a n)") for a in range(2)]
                rest_of_stage(0, NW, i + 1, chunk[1], chunk[0])
                add_bias0(i + 1, 0)
                make_x1(i, 1)
                add_bias0(i + 1, 1)
            last = PAIRS - 1

            make_x1(last, 0)
            rest_of_stage(0, NW, L8, early[:, 1, L8 - 1, :], early[:, 0, L8 - 1, :])
            make_x1(last, 1)
            for k in (0, 2):
                pool.wait_ge(late_hi, k + 1)
                hi, lo = (wlate_s[:, a, 2 * k:2 * k + 2, :].rearrange("p c n -> p (c n)") for a in range(2))
                g.tensor_tensor(lo, late_src[k], hi.bitcast(F32), ALU.subtract).then_inc(late_lo, 1)
            pool.wait_ge(bias1_loaded, 16)

            def add_bias1(i, p):
                pool.wait_ge(resid_loaded[p], 16 * (i + 1))
                g.tensor_tensor(resid[:, p, :], resid[:, p, :], bias_bc[:, :], ALU.add).then_inc(resid_ready, 1)

            with pool.Fori(0, PAIRS - 1) as i:
                for p in range(2):
                    add_bias1(i, p)
            add_bias1(last, 0)
            add_bias1(last, 1)


_INS = ["x", "consts", "rows", "mix", "wsign", "scales", "bias0", "toep", "wearly", "wlate", "bm", "bias1"]


def lay_out(a):
    import numpy as np
    f = {k: np.asarray(v) for k, v in a.items()}
    z = lambda *s: np.zeros(s, np.float32)
    perm = lambda w, axis: np.moveaxis(np.moveaxis(w, axis, -1).reshape(*np.moveaxis(w, axis, -1).shape[:-1], P, L8)
                                       .swapaxes(-1, -2).reshape(np.moveaxis(w, axis, -1).shape), -1, axis)
    turned = lambda w: w.reshape(w.shape[0], P, L8).transpose(1, 2, 0)
    consts = z(P, C_END)
    consts[:, C_W0:C_W0 + P] = f["L0_cond_W0"]
    consts[:, C_W1:C_W1 + P] = f["L0_cond_W1"]
    consts[:, C_W2:C_W2 + K8] = f["L0_cond_W2"]
    consts[:, C_CW:C_CW + S] = f["L1_cond_c_weight"].T
    consts[:, C_CT:C_CT + B] = f["cond_128"].T
    consts[:, C_B0] = f["L0_cond_b0"]
    consts[:, C_B1] = f["L0_cond_b1"]
    consts[:, C_GATE:C_GATE + L8 * E] = turned(f["L0_ffn_gate_w"]).reshape(P, L8 * E)
    consts[:, C_ID:C_ID + P] = np.eye(P, dtype=np.float32)
    rows = z(64, R_END)
    rows[0:B, R_B2:R_B2 + K8] = f["L0_cond_b2"]
    rows[0:B, R_FS:R_FS + S] = f["fside_S_0"]
    rows[0:K8, R_BK:R_BK + S] = f["L0_cond_bias_k"]
    is_lo = (np.arange(64) // E) % 2
    rows[:, R_LO] = is_lo
    rows[:, R_SG] = 1 - 2 * is_lo
    batch = np.arange(B)[:, None]
    rows[0:B, R_HALF:R_HALF + P] = batch % 2 == np.arange(P)[None] // S
    rows[0:B, R_TILE:R_TILE + P] = batch // 2 == np.arange(P)[None] // K8
    mix = np.tile(f["L0_cond_weight"].reshape(K8, S, S).transpose(2, 1, 0), (2, 1, 1))
    scales = np.concatenate([np.tile(perm(f["L0_ffn_in_channel_scale"], 1), (4, 1)),
                             np.tile(perm(f["L0_ffn_out_channel_scale"], 1), (4, 1))])
    wsign = turned(perm(f["L0_ffn_weight"], 0))
    cw = f["L1_cond_weight"].reshape(GROUPS, CG, CG, TAPS)
    toep = z(2, L8, CG, GROUPS, L8, CG)
    for l in range(L8):
        for k in range(TAPS):
            m = l + k
            toep[m // L8, m % L8, :, :, l, :] = cw[:, :, :, k].transpose(2, 0, 1)
    toep = toep.transpose(1, 2, 0, 3, 4, 5).reshape(P, 2 * GROUPS * P)
    w1 = turned(perm(f["L1_ffn_W"], 0))
    wearly = np.concatenate([turned(f["L1_ffn_Wq"]), turned(f["L1_ffn_Wk"]),
                             turned(f["L1_ffn_A"].reshape(NA, H)), w1[:, :, 0:HALF]], axis=2)
    bm = perm(f["L1_ffn_Bm"], 1).transpose(0, 2, 1).reshape(NA, H)
    return dict(x=perm(f["x"], 2).reshape(TILES * P, H), consts=consts, rows=rows, mix=mix, wsign=wsign,
                scales=scales, bias0=perm(f["L0_ffn_bias"], 0)[None], toep=toep, wearly=wearly,
                wlate=w1[:, :, HALF:], bm=bm, bias1=perm(f["L1_ffn_b"], 0)[None])


def kernel(**inputs):
    import numpy as np
    import concourse.bacc as bacc
    from concourse.bass_utils import run_bass_kernel_spmd

    nc = bacc.Bacc("TRN2", target_bir_lowering=False, num_devices=1)
    given = lay_out(inputs)
    arrays, args = {}, []
    for name in _INS:
        a = np.ascontiguousarray(given[name])
        arrays[f"in_{name}"] = a
        args.append(nc.dram_tensor(f"in_{name}", a.shape, mybir.dt.from_np(a.dtype), kind="ExternalInput").ap())
    out = nc.dram_tensor("out_tokens", (TILES * P, H), F32, kind="ExternalOutput").ap()
    adaln_ffn_kernel(nc, *args, out)
    r = run_bass_kernel_spmd(nc, [arrays], core_ids=[0])
    got = r.results[0]["out_tokens"]
    return got.reshape(B, S, L8, P).swapaxes(2, 3).reshape(B, S, H)
```
